# Optimizing a Trainium2 kernel written in Bass

```python
import numpy as np
import jax
import jax.numpy as jnp

def _softmax(x, axis=-1):
    return jax.nn.softmax(x, axis=axis)

def _gelu(x):
    return jax.nn.gelu(x, approximate=True)

def _silu(x):
    return jax.nn.silu(x)

def _sigmoid(x):
    return jax.nn.sigmoid(x)

def _layernorm(x, axis=-1, eps=1e-05):
    m = jnp.mean(x, axis=axis, keepdims=True)
    v = jnp.var(x, axis=axis, keepdims=True)
    return (x - m) / jnp.sqrt(v + eps)

def _scatter_add(tgt, idx, src, axis=0):
    return tgt.at[idx].add(src)

def _segment_sum(src, seg, n):
    return jax.ops.segment_sum(src, seg, n)
kernel_name = 'mk_gnn_preln_d2_gnn_r8_077df8'

def setup_inputs(seed: int=0):
    np.random.seed(seed)
    _w = jnp.asarray

    def _rec_inputs():
        import jax
        import jax.numpy as jnp
        _gk = jax.random.key(seed)
        x = -0.0002117 + 1 * jax.random.normal(jax.random.fold_in(_gk, 1), (6250, 256), jnp.float32)
        _s = jax.random.randint(jax.random.fold_in(_gk, 2), (100000,), 0, 6250, jnp.int32)
        _d = jax.random.randint(jax.random.fold_in(_gk, 3), (100000,), 0, 6250, jnp.int32)
        _loop = jnp.arange(6250, dtype=jnp.int32)
        src = jnp.concatenate([_s, _d, _loop])
        dst = jnp.concatenate([_d, _s, _loop])
        _o = jnp.argsort(dst, stable=True)
        src = src[_o]
        dst = dst[_o]
        edge_attr_10 = jax.random.uniform(jax.random.fold_in(_gk, 13), (206250, 10), jnp.float32, 0.0, 1)
        edge_attr_4 = 0.00109026 + 0.999989 * jax.random.normal(jax.random.fold_in(_gk, 14), (206250, 4), jnp.float32)
        edge_weight = jax.random.uniform(jax.random.fold_in(_gk, 15), (206250,), jnp.float32, 0.0, 1)
        return (x, src, dst, edge_attr_10, edge_attr_4, edge_weight)
    x, src, dst, edge_attr_10, edge_attr_4, edge_weight = _rec_inputs()

    def _L0_gnn_setup():
        import jax, jax.numpy as jnp
        import numpy as np
        BN_EPS = 1e-05

        def _batchnorm(h, gamma, beta):
            mean = jnp.mean(h, axis=0, keepdims=True)
            var = jnp.var(h, axis=0, keepdims=True)
            return (h - mean) * jax.lax.rsqrt(var + BN_EPS) * gamma + beta
        key = jax.random.key(seed)
        ks = jax.random.split(key, 10)
        N, E, D = (12500, 400000, 256)
        x = jax.random.normal(ks[0], (N, D), dtype=jnp.float32)
        edge_src = jax.random.randint(ks[1], (E,), 0, N, dtype=jnp.int32)
        edge_dst = jax.random.randint(ks[2], (E,), 0, N, dtype=jnp.int32)
        edge_vals = jnp.ones((E,), dtype=jnp.float32)
        n_norm = jax.random.uniform(ks[3], (N, 1), dtype=jnp.float32)
        s = 1.0 / np.sqrt(D)
        w1 = jax.random.uniform(ks[4], (D, D), jnp.float32, -s, s)
        gamma1 = jnp.ones((D,), jnp.float32)
        beta1 = jnp.zeros((D,), jnp.float32)
        w2 = jax.random.uniform(ks[5], (D, D), jnp.float32, -s, s)
        eps_weight = jnp.zeros((1,), jnp.float32)
        gamma_h = jnp.ones((D,), jnp.float32)
        beta_h = jnp.zeros((D,), jnp.float32)
        return {'x': x, 'edge_src': edge_src, 'edge_dst': edge_dst, 'edge_vals': edge_vals, 'n_norm': n_norm, 'w1': w1, 'gamma1': gamma1, 'beta1': beta1, 'w2': w2, 'eps_weight': eps_weight, 'gamma_h': gamma_h, 'beta_h': beta_h}
    _L0_gnn_all = _L0_gnn_setup()
    _L0_gnn_in = {k: v for k, v in _L0_gnn_all.items() if k in ('w1', 'gamma1', 'beta1', 'w2', 'eps_weight', 'gamma_h', 'beta_h')}
    del _L0_gnn_all

    def _L1_gnn_setup():
        import jax, jax.numpy as jnp
        import numpy as np
        MUL = 64
        N_NODES = 6250
        N_EDGES = 100000
        NUM_NEIGHBORS = 16.0
        SILU_NORM = 1.679177
        key = jax.random.key(seed)
        ks = jax.random.split(key, 9)
        node_in = jax.random.normal(ks[0], (N_NODES, 4 * MUL), dtype=jnp.float32)
        edge_src = jax.random.randint(ks[1], (N_EDGES,), 0, N_NODES)
        edge_dst = jax.random.randint(ks[2], (N_EDGES,), 0, N_NODES)
        edge_attr = jax.random.normal(ks[3], (N_EDGES, 4), dtype=jnp.float32)
        edge_len_emb = jax.random.uniform(ks[4], (N_EDGES, 10), dtype=jnp.float32)
        w_00_0 = jax.random.normal(ks[5], (MUL, MUL), dtype=jnp.float32)
        w_11_0 = jax.random.normal(ks[6], (MUL, MUL), dtype=jnp.float32)
        w_01_1 = jax.random.normal(ks[7], (MUL, MUL), dtype=jnp.float32)
        w_10_1 = jax.random.normal(ks[8], (MUL, MUL), dtype=jnp.float32)
        kf = jax.random.split(jax.random.fold_in(key, 1), 2)
        fc_w1 = jax.random.normal(kf[0], (10, 64), dtype=jnp.float32)
        fc_w2 = jax.random.normal(kf[1], (64, 1), dtype=jnp.float32)
        return {'node_in': node_in, 'edge_attr': edge_attr, 'edge_len_emb': edge_len_emb, 'w_00_0': w_00_0, 'w_11_0': w_11_0, 'w_01_1': w_01_1, 'w_10_1': w_10_1, 'fc_w1': fc_w1, 'fc_w2': fc_w2, 'edge_src': edge_src, 'edge_dst': edge_dst}
    _L1_gnn_all = _L1_gnn_setup()
    _L1_gnn_in = {k: v for k, v in _L1_gnn_all.items() if k in ('w_00_0', 'w_11_0', 'w_01_1', 'w_10_1', 'fc_w1', 'fc_w2')}
    del _L1_gnn_all
    return {'x': x, 'src': src, 'dst': dst, 'edge_attr_10': edge_attr_10, 'edge_attr_4': edge_attr_4, 'edge_weight': edge_weight, 'L0_gnn_w1': _L0_gnn_in['w1'], 'L0_gnn_gamma1': _L0_gnn_in['gamma1'], 'L0_gnn_beta1': _L0_gnn_in['beta1'], 'L0_gnn_w2': _L0_gnn_in['w2'], 'L0_gnn_eps_weight': _L0_gnn_in['eps_weight'], 'L0_gnn_gamma_h': _L0_gnn_in['gamma_h'], 'L0_gnn_beta_h': _L0_gnn_in['beta_h'], 'L1_gnn_w_00_0': _L1_gnn_in['w_00_0'], 'L1_gnn_w_11_0': _L1_gnn_in['w_11_0'], 'L1_gnn_w_01_1': _L1_gnn_in['w_01_1'], 'L1_gnn_w_10_1': _L1_gnn_in['w_10_1'], 'L1_gnn_fc_w1': _L1_gnn_in['fc_w1'], 'L1_gnn_fc_w2': _L1_gnn_in['fc_w2']}

def reference(x, src, dst, edge_attr_10, edge_attr_4, edge_weight, L0_gnn_w1, L0_gnn_gamma1, L0_gnn_beta1, L0_gnn_w2, L0_gnn_eps_weight, L0_gnn_gamma_h, L0_gnn_beta_h, L1_gnn_w_00_0, L1_gnn_w_11_0, L1_gnn_w_01_1, L1_gnn_w_10_1, L1_gnn_fc_w1, L1_gnn_fc_w2):
    import jax
    import jax.numpy as jnp

    def _L0_gnn_ref(x, edge_src, edge_dst, edge_vals, n_norm, w1, gamma1, beta1, w2, eps_weight, gamma_h, beta_h):
        import jax, jax.numpy as jnp
        import numpy as np
        BN_EPS = 1e-05

        def _batchnorm(h, gamma, beta):
            mean = jnp.mean(h, axis=0, keepdims=True)
            var = jnp.var(h, axis=0, keepdims=True)
            return (h - mean) * jax.lax.rsqrt(var + BN_EPS) * gamma + beta
        N = x.shape[0]
        msgs = edge_vals[:, None] * x[edge_src]
        agg = jax.ops.segment_sum(msgs, edge_dst, num_segments=N)
        y = agg + eps_weight * x
        h = jax.nn.relu(_batchnorm(y @ w1.T, gamma1, beta1))
        y = h @ w2.T
        y = y * n_norm
        y = _batchnorm(y, gamma_h, beta_h)
        y = jax.nn.relu(y)
        y = y + x
        return y

    def _L1_gnn_ref(node_in, edge_attr, edge_len_emb, w_00_0, w_11_0, w_01_1, w_10_1, fc_w1, fc_w2, edge_src, edge_dst):
        import jax, jax.numpy as jnp
        import numpy as np
        MUL = 64
        N_NODES = 6250
        N_EDGES = 100000
        NUM_NEIGHBORS = 16.0
        SILU_NORM = 1.679177
        src = node_in[edge_src]
        s0 = src[:, :MUL]
        s1 = src[:, MUL:].reshape(-1, MUL, 3)
        a0 = edge_attr[:, 0:1]
        a1 = edge_attr[:, 1:4]
        alpha = np.float32(1.0 / np.sqrt(2.0 * MUL))
        inv_sqrt3 = np.float32(1.0 / np.sqrt(3.0))
        out0 = alpha * (jnp.einsum('ei,io->eo', s0 * a0, w_00_0) + inv_sqrt3 * jnp.einsum('eim,em,io->eo', s1, a1, w_11_0))
        out1 = alpha * (jnp.einsum('ei,io,em->eom', s0, w_01_1, a1) + jnp.einsum('eim,io->eom', s1 * a0[:, :, None], w_10_1))
        msg_ang = jnp.concatenate([out0, out1.reshape(-1, 3 * MUL)], axis=1)
        h = jax.nn.silu(edge_len_emb @ fc_w1 / np.float32(np.sqrt(10.0))) * np.float32(SILU_NORM)
        msg_rad = h @ fc_w2 / np.float32(np.sqrt(64.0))
        messages = msg_ang * msg_rad
        agg = jax.ops.segment_sum(messages, edge_dst, num_segments=node_in.shape[0])
        return agg / np.float32(np.sqrt(NUM_NEIGHBORS))
    deg = jnp.maximum(jax.ops.segment_sum(jnp.ones(dst.shape, jnp.float32), dst, num_segments=6250), 1.0)
    deg_isqrt = deg ** (-0.5)
    h = jnp.maximum(_layernorm(x, axis=-1), 0.0)
    x = x + _L0_gnn_ref(h, src, dst, edge_weight, deg_isqrt[:, None], L0_gnn_w1, L0_gnn_gamma1, L0_gnn_beta1, L0_gnn_w2, L0_gnn_eps_weight, L0_gnn_gamma_h, L0_gnn_beta_h)
    h = jnp.maximum(_layernorm(x, axis=-1), 0.0)
    x = x + _L1_gnn_ref(h, edge_attr_4, edge_attr_10, L1_gnn_w_00_0, L1_gnn_w_11_0, L1_gnn_w_01_1, L1_gnn_w_10_1, L1_gnn_fc_w1, L1_gnn_fc_w2, src, dst)
    return x

_drawn_inputs = setup_inputs


def setup_inputs(seed=0):
    import zlib

    import numpy as np

    out = dict(_drawn_inputs(seed))
    spreads = {'L0_gnn_gamma1': (1.0, 0.2),
     'L0_gnn_beta1': (0.0, 0.1),
     'L0_gnn_gamma_h': (1.0, 0.2),
     'L0_gnn_beta_h': (0.0, 0.1)}
    factors = {}
    for name, (base, spread) in spreads.items():
        noise = np.random.default_rng([zlib.crc32(name.encode()), seed]).standard_normal(out[name].shape)
        drawn = base * np.exp(spread * noise) if base else spread * noise
        out[name] = jnp.asarray(drawn.astype(out[name].dtype))
    for name, factor in factors.items():
        out[name] = (out[name] * factor).astype(out[name].dtype)
    return out
```

```python
import concourse.bass as bass
from concourse import mybir
from concourse.alu_op_type import AluOpType as ALU
from contextlib import ExitStack

N, E, D, MUL = 6250, 206250, 256, 64
P = 128
J = 4
SB_EDGES = P * J
SLOTS = 4
SB = -(-(-(-E // SB_EDGES)) // SLOTS) * SLOTS
STEPS = SB // SLOTS
W = 32
PAIRS = -(-N // (2 * P))
NPAD = PAIRS * 2 * P
FAR = 8192
CH = 400
NCH = NPAD // CH
LAST = N - (NCH - 1) * CH
EMB, HID = 10, 64
KROUND = 256
EPS = 1e-5
SILU_NORM = 1.679177
NEIGHBOURS = 16.0
DST_TILES = -(-SB // P)

f32, i32, bf16 = mybir.dt.float32, mybir.dt.int32, mybir.dt.bfloat16
ACT = mybir.ActivationFunctionType
AX = mybir.AxisListType


class Memory:

    def __init__(self, nc, ctx):
        def sb(name, shape, dt=f32):
            return ctx.enter_context(nc.sbuf_tensor(name, shape, dt))

        def dram(name, shape):
            return nc.dram_tensor(name, shape, f32).ap()

        self.big = sb("big", [P, 5 * NPAD])
        self.acc = self.big[:, :].rearrange("p (k n) -> p k n", k=5)
        self.agg3 = self.big[:, 0:3 * NPAD].rearrange("p (k n) -> p k n", k=3)
        self.deg = self.agg3[:, 2, :]
        at = [3 * NPAD]

        def part(n):
            at[0] += n
            assert at[0] <= 5 * NPAD
            return self.big[:, at[0] - n:at[0]]

        self.w_edge = part((SB + 1) * J)
        self.radial = part(SB * J)
        self.w1T = part(2 * D).rearrange("p (k o) -> p k o", k=2)
        self.w2T = part(2 * D).rearrange("p (k o) -> p k o", k=2)
        self.emb = part(SLOTS * P).rearrange("p (u e) -> p u e", u=SLOTS)
        self.hid = part(2 * 2 * P).rearrange("p (b q e) -> p b q e", b=2, q=2)
        self.fc1 = part(4 * HID)
        self.sel0 = part(2 * J * W).rearrange("p (b j n) -> p b j n", b=2, j=J)
        self.agg_sb0 = part(2 * D).rearrange("p (b f) -> p b f", b=2)
        self.dstn = part(SB_EDGES)
        self.dstv = part(SB_EDGES)
        self.diag = part(4 * P).rearrange("p (b n) -> p b n", b=4)

        self.rows = sb("rows", [P, SLOTS, J, D])
        self.idx = sb("idx", [P, SLOTS, J], i32)
        pair = self.rows[:, :, :, :].rearrange("p (a b) (c t) f -> p a b c t f", a=2, c=2)
        self.tile_in = pair[:, 0, 0]
        self.tile_mid = pair[:, 0, 1]
        self.tile_out = pair[:, 1, 0]
        self.tile_aux = pair[:, 1, 1]
        self.rel = sb("rel", [P, SB + 1, J])
        self.coef = sb("coef", [P, SB + 1, J, 4])
        self.sel = sb("sel", [P, 2, J, 4, W])
        self.stage = self.coef[:, 0:2 * 5 * 2 * P // (4 * J), :, :].rearrange("p (b x) j c -> p b (x j c)", b=2)\
            .rearrange("p b (k n) -> p b k n", k=5)
        self.maskf = sb("maskf", [P, 2, J, W])
        self.maskb = sb("maskb", [P, 2, J, W], bf16)
        self.agg_sb = sb("agg_sb", [P, 2, D + MUL])
        self.base_bc = sb("base_bc", [P, DST_TILES * P])
        self.base_f = sb("base_f", [1, SB])
        self.base_i = sb("base_i", [1, SB], i32)
        self.rounds_i = sb("rounds_i", [1, 1], i32)
        self.iota0 = sb("iota0", [P, W])
        self.iota = sb("iota", [P, W])
        self.wk = sb("wk", [P, 5, D])
        self.fc2 = sb("fc2", [P, 2])
        self.ident = sb("ident", [P, P])
        self.ones = sb("ones", [P, P])
        self.ones_b = sb("ones_b", [P, P], bf16)
        self.bn_par = sb("bn_par", [P, 4, 2])
        self.eps_w = sb("eps_w", [P, 1])
        self.stats = sb("stats", [P, 2, NCH, 6])
        self.mv = sb("mv", [P, 2, 2])
        self.scale = sb("scale", [P, 2])
        self.shift = sb("shift", [P, 2])
        self.tmp2 = sb("tmp2", [P, 2])
        self.st6 = sb("st6", [P, 2, 2, 6])
        self.tmv = sb("tmv", [P, 2, 2, 2])
        self.rstd = sb("rstd", [P, 2, 2])
        self.nmr = sb("nmr", [P, 2, 2])
        self.std = sb("std", [P, 2, 2])
        self.eps_bn = sb("eps_bn", [P, 1])
        self.colmin = sb("colmin", [P, DST_TILES])
        self.colspan = sb("colspan", [P, DST_TILES])
        self.spanmax = sb("spanmax", [P, 1])
        self.thresh = sb("thresh", [P, KROUND])
        self.rounds_f = sb("rounds_f", [P, 1])

        self.ps = [ctx.enter_context(nc.psum_tensor(f"bank{i}", [P, 512], f32)) for i in range(8)]

        self.h_tab = dram("h_tab", [NPAD, D])
        self.xh_tab = dram("xh_tab", [NPAD, D])
        self.x2_tab = dram("x2_tab", [NPAD, D])
        self.h2_tab = dram("h2_tab", [NPAD, D])


def sems(nc, ctx, *names):
    return [ctx.enter_context(nc.semaphore(n)) for n in names]


def pair_rows(table, i):
    return table[bass.ds(i * (2 * P), 2 * P), :].rearrange("(a p) f -> p a f", p=P)


def constants(nc, m, w):
    ctx = ExitStack()
    with ctx:
        zeroed, loaded, ident0, ramp, done = sems(nc, ctx, "c_zeroed", "c_loaded", "c_ident0", "c_ramp", "c_done")
        block = ctx.enter_context(nc.Block())
        alpha = (2.0 * MUL) ** -0.5
        n_dma = 2 + 4 + 1 + 4 + 2 + 10 + 3

        @block.sync
        def _(sp):
            def load(out, in_):
                sp.dma_start(out, in_).then_inc(loaded, 16)

            load(m.w1T, w["w1T"].rearrange("(k p) o -> p k o", p=P))
            load(m.w2T, w["w2T"].rearrange("(k p) o -> p k o", p=P))
            for k, name in enumerate(("gamma1", "beta1", "gamma_h", "beta_h")):
                load(m.bn_par[:, k, :], w[name])
            load(m.eps_w[:, :], w["eps"].to_broadcast([P, 1]))
            load(m.w_edge, w["edge_weight"])
            load(m.coef[:, :, :, :].rearrange("p t j c -> p (t j c)"), w["edge_attr_4"])
            load(m.rel[:, :, :].rearrange("p t j -> p (t j)").bitcast(i32), w["dst_slots"])
            sp.wait_ge(zeroed, 4)
            for j in range(J):
                load(m.fc1[EMB * j:EMB * (j + 1), HID * j:HID * (j + 1)], w["fc_w1"])
            load(m.fc2[0:HID, 0:1], w["fc_w2"])
            load(m.fc2[HID:P, 1:2], w["fc_w2"])
            lo, hi = slice(0, MUL), slice(MUL, P)
            for k, part, col, name in ((0, lo, 2, "w_10_1"), (0, hi, 3, "w_10_1"),
                                       (1, lo, 0, "w_11_0"), (1, hi, 1, "w_01_1"),
                                       (2, lo, 2, "w_01_1"), (2, hi, 0, "w_11_0"),
                                       (3, lo, 0, "w_11_0"), (3, hi, 3, "w_01_1"),
                                       (4, lo, 1, "w_10_1"), (4, hi, 0, "w_00_0")):
                load(m.wk[part, k, MUL * col:MUL * (col + 1)], w[name])
            sp.wait_ge(loaded, 16 * (n_dma - 0 - 0))

        @block.gpsimd
        def _(pool):
            nc.gpsimd.memset(m.fc1, 0.0).then_inc(zeroed, 1)
            nc.gpsimd.memset(m.fc2[:, :], 0.0).then_inc(zeroed, 1)
            nc.gpsimd.memset(m.wk[:, :, :], 0.0).then_inc(zeroed, 1)
            nc.gpsimd.memset(m.ones[:, :], 1.0).then_inc(zeroed, 1)
            nc.gpsimd.memset(m.ones_b[:, :], 1.0)
            nc.gpsimd.memset(m.eps_bn[:, :], EPS)
            nc.gpsimd.memset(m.deg, 0.0)
            nc.gpsimd.memset(m.ident[:, :], 0.0).then_inc(ident0, 1)
            pool.wait_ge(ident0, 1)
            nc.gpsimd.affine_select(out=m.ident[:, :], in_=m.ident[:, :], compare_op=ALU.not_equal, fill=1.0,
                                    base=0, pattern=[[-1, P]], channel_multiplier=1)
            nc.gpsimd.iota(m.iota0[:, :], pattern=[[1, W]], base=0, channel_multiplier=0,
                           allow_small_or_imprecise_dtypes=True)
            nc.gpsimd.iota(m.thresh[:, :], pattern=[[W, KROUND]], base=W, channel_multiplier=0,
                           allow_small_or_imprecise_dtypes=True)

        @block.vector
        def _(dve):
            dve.wait_ge(loaded, 16 * n_dma)
            nc.vector.tensor_scalar_mul(m.fc2[:, :], m.fc2[:, :], SILU_NORM / HID ** 0.5 / NEIGHBOURS ** 0.5)
            for k in range(5):
                last = nc.vector.tensor_scalar_mul(m.wk[:, k, :], m.wk[:, k, :], alpha)
            last.then_inc(done, 1)
            dve.wait_ge(done, 1)
            for k, part in ((1, slice(0, MUL)), (2, slice(MUL, P)), (3, slice(0, MUL))):
                nc.vector.tensor_scalar_mul(m.wk[part, k, 0:MUL], m.wk[part, k, 0:MUL], 3.0 ** -0.5)
            nc.vector.tensor_copy(m.rel[:, :, :].rearrange("p t j -> p (t j)"),
                                  m.rel[:, :, :].rearrange("p t j -> p (t j)").bitcast(i32))


def windows(nc, m, dst_rows):
    ctx = ExitStack()
    with ctx:
        landed, chain, spread, zeroed = sems(nc, ctx, "w_landed", "w_chain", "w_spread", "w_zeroed")
        block = ctx.enter_context(nc.Block())
        spans, bases = m.ps[0], m.ps[1]

        @block.sync
        def _(sp):
            for k in range(DST_TILES):
                rows = min(P, SB - P * k)
                if k:
                    sp.wait_ge(chain, 4 * k + 1)
                sp.dma_start(m.dstn[0:rows, :].bitcast(i32), dst_rows[P * k:P * k + rows, :]).then_inc(landed, 16)

        @block.vector
        def _(dve):
            steps = [0]

            def link(ins):
                steps[0] += 1
                ins.then_inc(chain, 1)
                dve.wait_ge(chain, steps[0])

            nc.vector.memset(m.colmin[:, :], 0.0)
            link(nc.vector.memset(m.colspan[:, :], 0.0))
            for k in range(DST_TILES):
                rows = min(P, SB - P * k)
                dve.wait_ge(landed, 16 * (k + 1))
                link(nc.vector.tensor_copy(m.dstv[0:rows, :], m.dstn[0:rows, :].bitcast(i32)))
                link(nc.vector.tensor_reduce(m.colmin[0:rows, k:k + 1], m.dstv[0:rows, :], AX.X, ALU.min))
                link(nc.vector.scalar_tensor_tensor(m.dstn[0:rows, :], m.dstv[0:rows, :], float(FAR), m.dstv[0:rows, :],
                                                    ALU.is_lt, ALU.mult))
                link(nc.vector.tensor_reduce(m.colspan[0:rows, k:k + 1], m.dstn[0:rows, :], AX.X, ALU.max))
            link(nc.vector.tensor_tensor(m.colspan[:, :], m.colspan[:, :], m.colmin[:, :], ALU.subtract))
            for k in range(DST_TILES):
                nc.vector.tensor_scalar(m.diag[:, k, :], m.ident[:, :], m.colspan[:, k:k + 1], None, ALU.mult)
                last = nc.vector.tensor_scalar(m.big[:, 0:DST_TILES * P].rearrange("p (k n) -> p k n", k=DST_TILES)[:, k, :],
                                               m.ident[:, :], m.colmin[:, k:k + 1], None, ALU.mult)
            last.then_inc(spread, 1)
            dve.wait_ge(spread, 2)
            link(nc.vector.tensor_scalar_min(m.base_bc[:, :], bases[:, 0:DST_TILES * P], float(NPAD - W)))
            link(nc.vector.tensor_reduce(m.spanmax[:, :], spans[:, 0:DST_TILES * P], AX.X, ALU.max))
            link(nc.vector.tensor_scalar(m.thresh[:, :], m.thresh[:, :], m.spanmax[:, 0:1], None, ALU.is_le))
            link(nc.vector.tensor_reduce(m.rounds_f[:, :], m.thresh[:, :], AX.X, ALU.add))
            nc.vector.tensor_scalar_add(m.rounds_i[0:1, :], m.rounds_f[0:1, :], 1.0)
            link(nc.vector.tensor_tensor(m.rel[:, 0:SB, :], m.rel[:, 0:SB, :],
                                         m.base_bc[:, 0:SB].unsqueeze(2).to_broadcast([P, SB, J]), ALU.subtract))
            nc.vector.tensor_scalar_add(m.rel[:, SB, :], m.rel[:, 0, :], -float(W))

        @block.tensor
        def _(pe):
            pe.wait_ge(spread, 1)
            nc.tensor.matmul(spans[:, 0:DST_TILES * P], m.ones[:, :], m.diag[:, :, :].rearrange("p k n -> p (k n)"),
                             start=True, stop=True)
            nc.tensor.matmul(bases[:, 0:DST_TILES * P], m.ones[:, :], m.big[:, 0:DST_TILES * P],
                             start=True, stop=True).then_inc(spread, 1)


def node_pairs(eng, step):
    half = PAIRS // 2
    assert PAIRS % 2 == 1
    step(0, 0, 0, True)
    step(1, 1, 0, True)
    with eng.Fori(1, half) as s:
        for b in range(2):
            step(2 * s + b, b, s, False)
    step(PAIRS - 1, 0, half, False)


def moments(nc, m, dve, chain, var_ready, std_ready, ready, mark, i, b, src, factors_read):
    nc.vector.bn_stats(m.st6[:, b, 0, :], src[:, 0, :])
    nc.vector.bn_stats(m.st6[:, b, 1, :], src[:, 1, :]).then_inc(chain, 1)
    dve.wait_ge(chain, 2 * i + 1)
    dve.sem_inc(mark, 1)
    nc.vector.bn_aggr(m.tmv[:, b, 0, :], m.st6[:, b, 0, :])
    nc.vector.bn_aggr(m.tmv[:, b, 1, :], m.st6[:, b, 1, :]).then_inc(var_ready, 1)
    if factors_read is not None:
        dve.wait_ge(factors_read, i - 1)
    dve.wait_ge(std_ready, i + 1)
    nc.vector.reciprocal(m.rstd[:, b, :], m.std[:, b, :]).then_inc(chain, 1)
    dve.wait_ge(chain, 2 * i + 2)
    nc.vector.scalar_tensor_tensor(m.nmr[:, b, :], m.tmv[:, b, :, 0], -1.0, m.rstd[:, b, :],
                                   ALU.mult, ALU.mult).then_inc(ready, 1)


def root(nc, m, act, var_ready, std_ready, i, b):
    act.wait_ge(var_ready, i + 1)
    nc.scalar.activation(m.std[:, b, :], m.tmv[:, b, :, 1], ACT.Sqrt, bias=m.eps_bn[:, 0:1]).then_inc(std_ready, 1)


def input_norm(nc, m, x):
    ctx = ExitStack()
    with ctx:
        x_in = sems(nc, ctx, "n_x_in0", "n_x_in1")
        out_s = sems(nc, ctx, "n_out0", "n_out1")
        chain, var_ready, std_ready, factors, h_ready, xh_ready, hT_ready, hT_free = sems(
            nc, ctx, "n_chain", "n_var", "n_std", "n_factors", "n_h", "n_xh", "n_hT", "n_hT_free")
        mark_a, mark_d, mark_pe, mark_p = sems(nc, ctx, "n_mark_a", "n_mark_d", "n_mark_pe", "n_mark_p")
        block = ctx.enter_context(nc.Block())

        @block.sync
        def _(sp):
            def step(i, b, s, first):
                if not first:
                    sp.wait_ge(xh_ready, i - 1)
                sp.dma_start(m.tile_in[:, b], pair_rows(x, i)).then_inc(x_in[b], 16)
            node_pairs(sp, step)

        @block.vector
        def _(dve):
            def step(i, b, s, first):
                dve.wait_ge(x_in[b], 16 * s + 16)
                moments(nc, m, dve, chain, var_ready, std_ready, factors, mark_d, i, b, m.tile_in[:, b],
                        None if first else h_ready)
            node_pairs(dve, step)

        @block.scalar
        def _(act):
            def first_addend(i, b):
                act.wait_ge(hT_ready, i + 1)
                act.sem_inc(mark_a, 1)
                nc.scalar.activation(m.agg3[:, 0:2, bass.ds(i * (2 * P), 2 * P)],
                                     m.ps[b][:, :].rearrange("p (k n) -> p k n", k=2), ACT.Copy,
                                     scale=m.eps_w[:, 0:1]).then_inc(hT_free, 1)

            def step(i, b, s, first):
                root(nc, m, act, var_ready, std_ready, i, b)
                if not (first and i == 0):
                    first_addend(i - 1, 1 - b)
                act.wait_ge(factors, i + 1)
                if not first:
                    act.wait_ge(out_s[b], 32 * s)
                for a in range(2):
                    last = nc.scalar.activation(m.tile_mid[:, b, a, :], m.tile_in[:, b, a, :], ACT.Relu,
                                                bias=m.nmr[:, b, a:a + 1], scale=m.rstd[:, b, a:a + 1])
                last.then_inc(h_ready, 1)
            node_pairs(act, step)
            first_addend(PAIRS - 1, 0)

        @block.tensor
        def _(pe):
            def step(i, b, s, first):
                pe.wait_ge(h_ready, i + 1)
                if not first:
                    pe.wait_ge(hT_free, i - 1)
                pe.sem_inc(mark_pe, 1)
                for a in range(2):
                    for k in range(2):
                        last = nc.tensor.transpose(m.ps[b][:, 2 * P * k + P * a:2 * P * k + P * (a + 1)],
                                                   m.tile_mid[:, b, a, P * k:P * (k + 1)], m.ident[:, :])
                last.then_inc(hT_ready, 1)
            node_pairs(pe, step)

        @block.gpsimd
        def _(pool):
            def step(i, b, s, first):
                pool.wait_ge(h_ready, i + 1)
                if not first:
                    pool.wait_ge(out_s[b], 32 * s)
                pool.sem_inc(mark_p, 1)
                nc.gpsimd.tensor_tensor(m.tile_out[:, b], m.tile_in[:, b], m.tile_mid[:, b], ALU.add).then_inc(xh_ready, 1)
                pool.dma_start(pair_rows(m.h_tab, i), m.tile_mid[:, b]).then_inc(out_s[b], 16)
                pool.wait_ge(xh_ready, i + 1)
                pool.wait_ge(hT_ready, i + 1)
                pool.sem_inc(mark_p, 1)
                pool.dma_start(pair_rows(m.xh_tab, i), m.tile_out[:, b]).then_inc(out_s[b], 16)
            node_pairs(pool, step)
            pool.wait_ge(out_s[0], 32 * (PAIRS // 2 + 1))
            pool.wait_ge(out_s[1], 32 * (PAIRS // 2))


def superblocks(nc, eng, m, body):
    rounds = eng.value_load(m.rounds_i[0:1, 0:1], min_val=1, max_val=KROUND)
    with eng.Fori(0, rounds) as r:
        with eng.Fori(0, STEPS) as i:
            for u in range(SLOTS):
                body(r * SB + i * SLOTS + u, i * SLOTS + u, u, r * STEPS + i)


def sweep(nc, m, layer, table, idx_rows, emb_rows):
    first = layer == 1
    tag = f"e{layer}_"
    ctx = ExitStack()
    with ctx:
        names = ("idx_landed", "emb_landed", "rows_landed")
        idx_landed, emb_landed, rows_landed = (sems(nc, ctx, *(f"{tag}{n}{u}" for u in range(SLOTS))) for n in names)
        (sel_ready, sums_ready, sums_sb, sumsT_ready, added, hid_ready, hid_sb, rad_ready, rad_sb, chain, mask_ready,
         mark_d, mark_pe, mark_p, mark_s) = sems(nc, ctx, *(tag + n for n in (
             "sel_ready", "sums_ready", "sums_sb", "sumsT_ready", "added", "hid_ready", "hid_sb", "rad_ready",
             "rad_sb", "chain", "mask_ready", "mark_d", "mark_pe", "mark_p", "mark_s")))
        block = ctx.enter_context(nc.Block())
        width = W if first else 4 * W
        sums = [m.ps[b][0:width, 0:D] for b in range(2)]
        sumsT = [m.ps[2 + b][:, 0:3 * W] for b in range(2)]
        hidden = [m.ps[4 + b][:, 0:2 * P] for b in range(2)]
        radial = [m.ps[6 + b][:, 0:J] for b in range(2)]
        sums_out = [(m.agg_sb0 if first else m.agg_sb)[0:width, b, :] for b in range(2)]
        accs = m.agg3 if first else m.acc

        @block.sync
        def _(sp):
            def step(g, t, u, n):
                sp.wait_ge(sums_sb, g + 1)
                sp.sem_inc(mark_s, 1)
                sp.dma_start(m.idx[:, u, :], idx_rows[bass.ds(t, 1), :, :].rearrange("t p j -> p (t j)")).then_inc(idx_landed[u], 16)
                if first:
                    sp.wait_ge(hid_sb, g + 1)
                    sp.sem_inc(mark_s, 1)
                    sp.dma_start(m.emb[0:J * EMB, u, :], emb_rows[bass.ds(t, 1), :, :].rearrange("t k e -> k (t e)")).then_inc(emb_landed[u], 16)
            superblocks(nc, sp, m, step)

        @block.gpsimd
        def _(pool):
            def step(g, t, u, n):
                pool.wait_ge(idx_landed[u], 16 * n + 16)
                pool.sem_inc(mark_p, 1)
                for j in range(J):
                    pool.indirect_dma_start(out=m.rows[:, u, j, :], out_offset=None, in_=table,
                                            in_offset=bass.IndirectOffsetOnAxis(ap=m.idx[:, u, j:j + 1], axis=0),
                                            bounds_check=N - 1, oob_is_err=False).then_inc(rows_landed[u], 16)
            superblocks(nc, pool, m, step)

        @block.tensor
        def _(pe):
            def step(g, t, u, n):
                b = u % 2
                if first:
                    pe.wait_ge(emb_landed[u], 16 * n + 16)
                    pe.wait_ge(hid_sb, g + SLOTS - 1)
                    pe.sem_inc(mark_pe, 1)
                    for q in range(2):
                        last = nc.tensor.matmul(hidden[b][:, P * q:P * (q + 1)], m.fc1[0:J * EMB, P * q:P * (q + 1)],
                                                m.emb[0:J * EMB, u, :], start=True, stop=True)
                    last.then_inc(hid_ready, 1)
                pe.wait_ge(rows_landed[u], 16 * J * (n + 1))
                pe.wait_ge(sel_ready, g + 1)
                pe.wait_ge(sums_sb, g + SLOTS - 1)
                pe.sem_inc(mark_pe, 1)
                for j in range(J):
                    sel = m.sel0[:, b, j, :] if first else m.sel[:, b, j, :, :].rearrange("p c n -> p (c n)")
                    last = nc.tensor.matmul(sums[b], sel, m.rows[:, u, j, :], start=(j == 0), stop=(j == J - 1))
                last.then_inc(sums_ready, 1)
                if first:
                    pe.wait_ge(hid_sb, g + SLOTS + 1)
                    pe.wait_ge(rad_sb, g + 1)
                    pe.sem_inc(mark_pe, 1)
                    for q in range(2):
                        last = nc.tensor.matmul(radial[b][:, 2 * q:2 * q + 2], m.hid[:, b, q, :], m.fc2[:, :],
                                                start=True, stop=True)
                    last.then_inc(rad_ready, 1)
                pe.wait_ge(added, g + 1)
                pe.sem_inc(mark_pe, 1)
                if first:
                    for j in range(J):
                        nc.tensor.matmul(sumsT[b][:, 2 * W:3 * W], m.ones_b[:, :], m.maskb[:, b, j, :],
                                         start=(j == 0), stop=(j == J - 1))
                pe.wait_ge(sums_sb, g + SLOTS + 1)
                pe.sem_inc(mark_pe, 1)
                if first:
                    for k in range(2):
                        last = nc.tensor.transpose(sumsT[b][:, W * k:W * (k + 1)], sums_out[b][:, P * k:P * (k + 1)],
                                                   m.ident[0:W, 0:W])
                else:
                    for q, col in enumerate((2, 0, 1, 3)):
                        last = nc.tensor.transpose(m.ps[2 + b][:, P * q:P * (q + 1)],
                                                   sums_out[b][:, MUL * col:MUL * (col + 2)], m.ident[:, :])
                last.then_inc(sumsT_ready, 1)
            superblocks(nc, pe, m, step)

        @block.scalar
        def _(act):
            act.sem_inc(sums_sb, SLOTS)
            if first:
                act.sem_inc(hid_sb, SLOTS)

            def step(g, t, u, n):
                b = u % 2
                if first:
                    act.wait_ge(hid_ready, g + 1)
                    nc.scalar.activation(m.hid[:, b, :, :], hidden[b].rearrange("p (q e) -> p q e", q=2), ACT.Silu,
                                         scale=EMB ** -0.5).then_inc(hid_sb, 1)
                act.wait_ge(sums_ready, g + 1)
                if not first:
                    nc.scalar.activation(sums_out[b][:, D:D + MUL], sums[b][:, MUL:2 * MUL], ACT.Copy)
                nc.scalar.activation(sums_out[b][:, 0:D], sums[b], ACT.Copy).then_inc(sums_sb, 1)
            superblocks(nc, act, m, step)

        @block.vector
        def _(dve):
            dve.sem_inc(added, 2)
            dve.sem_inc(rad_sb, 2)

            def select(t, b, step, masks):
                mask = m.maskb[:, b] if first else m.maskf[:, b]
                rel = m.rel[:, bass.ds(t, 1), :].rearrange("p t j -> p (t j)")
                nc.vector.tensor_tensor(mask, m.iota[:, :].unsqueeze(1).to_broadcast([P, J, W]),
                                        rel.unsqueeze(2).to_broadcast([P, J, W]), ALU.is_equal).then_inc(mask_ready, 1)
                dve.wait_ge(mask_ready, masks + 1)
                if first:
                    w = m.w_edge[:, bass.ds(t * J, J)]
                    nc.vector.tensor_tensor(m.sel0[:, b], mask, w.unsqueeze(2).to_broadcast([P, J, W]),
                                            ALU.mult).then_inc(sel_ready, 1)
                else:
                    c = m.coef[:, bass.ds(t, 1), :, :].rearrange("p t j c -> p (t j) c")
                    nc.vector.tensor_tensor(m.sel[:, b], mask.unsqueeze(2).to_broadcast([P, J, 4, W]),
                                            c.unsqueeze(3).to_broadcast([P, J, 4, W]), ALU.mult).then_inc(sel_ready, 1)

            nc.vector.tensor_copy(m.iota[:, :], m.iota0[:, :])
            nc.vector.tensor_copy(m.base_f[:, :], m.base_bc[0:1, 0:SB])
            if not first:
                nc.vector.memset(m.acc[:, 0:2, :], 0.0)
            nc.vector.tensor_copy(m.base_i[:, :], m.base_bc[0:1, 0:SB]).then_inc(chain, 1)
            dve.wait_ge(chain, 1)
            select(0, 0, 0, 0)
            rounds = dve.value_load(m.rounds_i[0:1, 0:1], min_val=1, max_val=KROUND)
            with dve.Fori(0, rounds) as r:
                with dve.Fori(0, STEPS) as i:
                    for u in range(SLOTS):
                        g, t, b = r * SB + i * SLOTS + u, i * SLOTS + u, u % 2
                        base = dve.value_load(m.base_i[0:1, bass.ds(t, 1)], min_val=0, max_val=NPAD - W)
                        select(t + 1, 1 - b, g + 1, g + 1)
                        if first:
                            dve.wait_ge(rad_ready, g + 1)
                            dve.sem_inc(mark_d, 1)
                            nc.vector.tensor_copy(m.radial[:, bass.ds(t * J, J)], radial[b]).then_inc(rad_sb, 1)
                        dve.wait_ge(added, g + 2)
                        dve.wait_ge(sumsT_ready, g + 1)
                        if first:
                            new = sumsT[b].rearrange("p (k n) -> p k n", n=W)
                        else:
                            new = bass.AP(tensor=m.ps[2 + b], offset=0, ap=[[512, P], [P + W, 4], [1, W]])
                            window = m.acc[:, 4, bass.ds(base, W)]
                            nc.vector.tensor_tensor(window, window, m.ps[2 + b][:, P:P + W], ALU.add)
                        window = accs[:, 0:3 if first else 4, bass.ds(base, W)]
                        nc.vector.tensor_tensor(window, window, new, ALU.add).then_inc(added, 1)
                dve.wait_ge(sel_ready, (r + 1) * SB + 1)
                nc.vector.tensor_scalar_add(m.iota[:, :], m.iota[:, :], float(W))
                nc.vector.tensor_scalar(m.base_f[:, :], m.base_f[:, :], float(W), float(NPAD - W),
                                        ALU.add, ALU.min).then_inc(chain, 1)
                dve.wait_ge(chain, 2 * r + 2)
                nc.vector.tensor_copy(m.base_i[:, :], m.base_f[:, :]).then_inc(chain, 1)
                dve.wait_ge(chain, 2 * r + 3)


def product(nc, m, wT, stage, gamma, beta):
    ctx = ExitStack()
    with ctx:
        tag = f"p{stage}_"
        (in_ready, mm_ready, out_sb, chain, aggr, floor_done, var_ready, std_ready, mark_a, mark_d, mark_pe) = sems(nc, ctx, *(tag + n for n in (
            "in_ready", "mm_ready", "out_sb", "chain", "aggr", "floor_done", "var_ready", "std_ready", "mark_a", "mark_d", "mark_pe")))
        block = ctx.enter_context(nc.Block())
        banks = [[m.ps[2 * b + k][:, 0:CH] for k in range(2)] for b in range(2)]
        assert NCH % 2 == 0

        def chunks(eng, step):
            step(0, 0, True, CH)
            step(1, 1, True, CH)
            with eng.Fori(1, NCH // 2 - 1) as s:
                for b in range(2):
                    step(2 * s + b, b, False, CH)
            step(NCH - 2, 0, False, CH)
            step(NCH - 1, 1, False, LAST)

        @block.tensor
        def _(pe):
            def step(c, b, first, real):
                if stage == 2:
                    pe.wait_ge(in_ready, c + 1)
                if not first:
                    pe.wait_ge(out_sb, c - 1)
                pe.sem_inc(mark_pe, 1)
                for k in range(2):
                    for q in range(2):
                        last = nc.tensor.matmul(banks[b][k], wT[:, q, P * k:P * (k + 1)],
                                                m.agg3[:, q, bass.ds(c * CH, CH)], start=(q == 0), stop=(q == 1))
                last.then_inc(mm_ready, 1)
            chunks(pe, step)

        @block.scalar
        def _(act):
            def step(c, b, first, real):
                if stage == 1:
                    act.wait_ge(mm_ready, c + 1)
                    act.sem_inc(mark_a, 1)
                    for k in range(2):
                        last = nc.scalar.activation(m.agg3[:, k, bass.ds(c * CH, CH)], banks[b][k], ACT.Copy)
                    last.then_inc(in_ready, 1)
                else:
                    for k in range(2):
                        chunk = m.agg3[:, k, bass.ds(c * CH, CH)]
                        last = nc.scalar.activation(chunk, chunk, ACT.Relu, bias=m.shift[:, k:k + 1], scale=m.scale[:, k:k + 1])
                    last.then_inc(in_ready, 1)
            chunks(act, step)
            if stage == 1:
                act.wait_ge(floor_done, 1)
                nc.scalar.activation(m.deg, m.deg, ACT.Sqrt)
            act.wait_ge(var_ready, 1)
            nc.scalar.activation(m.tmp2[:, :], m.mv[:, :, 1], ACT.Sqrt, bias=m.eps_bn[:, 0:1]).then_inc(std_ready, 1)

        @block.vector
        def _(dve):
            if stage == 1:
                nc.vector.tensor_scalar_max(m.deg, m.deg, 1.0).then_inc(floor_done, 1)
            else:
                nc.vector.reciprocal(m.deg, m.deg).then_inc(floor_done, 1)
                dve.wait_ge(floor_done, 1)

            def step(c, b, first, real):
                if stage == 1:
                    dve.wait_ge(in_ready, c + 1)
                    dve.sem_inc(mark_d, 1)
                    for k in range(2):
                        last = nc.vector.bn_stats(m.stats[:, k, bass.ds(c, 1), :].rearrange("p c s -> p (c s)"), banks[b][k][:, 0:real])
                    last.then_inc(out_sb, 1)
                else:
                    dve.wait_ge(mm_ready, c + 1)
                    for k in range(2):
                        last = nc.vector.tensor_tensor(m.agg3[:, k, bass.ds(c * CH, CH)], banks[b][k],
                                                       m.deg[:, bass.ds(c * CH, CH)], ALU.mult)
                    last.then_inc(out_sb, 1)
                    dve.wait_ge(out_sb, c + 1)
                    dve.sem_inc(mark_d, 1)
                    for k in range(2):
                        last = nc.vector.bn_stats(m.stats[:, k, bass.ds(c, 1), :].rearrange("p c s -> p (c s)"),
                                                  m.agg3[:, k, bass.ds(c * CH, real)])
                    last.then_inc(chain, 1)
            chunks(dve, step)
            if stage == 1:
                dve.wait_ge(out_sb, NCH)
            else:
                dve.wait_ge(chain, NCH)
            for k in range(2):
                last = nc.vector.bn_aggr(m.mv[:, k, :], m.stats[:, k, :, :].rearrange("p c s -> p (c s)"))
            last.then_inc(var_ready, 1)
            dve.wait_ge(std_ready, 1)
            nc.vector.reciprocal(m.scale[:, :], m.tmp2[:, :]).then_inc(aggr, 1)
            dve.wait_ge(aggr, 1)
            nc.vector.tensor_tensor(m.scale[:, :], m.scale[:, :], m.bn_par[:, gamma, :], ALU.mult).then_inc(aggr, 1)
            dve.wait_ge(aggr, 2)
            nc.vector.tensor_tensor(m.tmp2[:, :], m.mv[:, :, 0], m.scale[:, :], ALU.mult).then_inc(aggr, 1)
            dve.wait_ge(aggr, 3)
            nc.vector.tensor_tensor(m.shift[:, :], m.bn_par[:, beta, :], m.tmp2[:, :], ALU.subtract)


def between(nc, m):
    ctx = ExitStack()
    with ctx:
        xh_in = sems(nc, ctx, "b_xh_in0", "b_xh_in1")
        out_s = sems(nc, ctx, "b_out0", "b_out1")
        relu_ready, turned, x2_ready, var_ready, std_ready, factors, h2_ready, chain, mark_pe, scaled_coef, mark_a, mark_d, mark_p = sems(
            nc, ctx, "b_relu", "b_turned", "b_x2", "b_var", "b_std", "b_factors", "b_h2", "b_chain", "b_mark_pe", "b_scaled_coef", "b_mark_a", "b_mark_d", "b_mark_p")
        block = ctx.enter_context(nc.Block())
        xh, relu, x2, h2 = m.tile_in, m.tile_mid, m.tile_out, m.tile_aux

        @block.sync
        def _(sp):
            def step(i, b, s, first):
                if not first:
                    sp.wait_ge(x2_ready, i - 1)
                sp.dma_start(xh[:, b], pair_rows(m.xh_tab, i)).then_inc(xh_in[b], 16)
            node_pairs(sp, step)

        @block.scalar
        def _(act):
            def step(i, b, s, first):
                if not first:
                    act.wait_ge(turned, i - 1)
                    act.sem_inc(mark_a, 1)
                for k in range(2):
                    last = nc.scalar.activation(relu[:, b, k, :], m.agg3[:, k, bass.ds(i * (2 * P), 2 * P)], ACT.Relu,
                                                bias=m.shift[:, k:k + 1], scale=m.scale[:, k:k + 1])
                last.then_inc(relu_ready, 1)
                if not (first and i == 0):
                    norm(i - 1, 1 - b)

            def norm(i, b):
                root(nc, m, act, var_ready, std_ready, i, b)
                act.wait_ge(factors, i + 1)
                for a in range(2):
                    vectors = x2[:, b, a, MUL:D].rearrange("p (i v) -> p v i", v=3)
                    for to, part in ((h2[:, b, a, MUL:2 * MUL], x2[:, b, a, 0:MUL]),
                                     (h2[:, b, a, 0:MUL], vectors[:, 0, :]),
                                     (h2[:, b, a, 2 * MUL:D].rearrange("p (v i) -> p v i", v=2), vectors[:, 1:3, :])):
                        last = nc.scalar.activation(to, part, ACT.Relu, bias=m.nmr[:, b, a:a + 1],
                                                    scale=m.rstd[:, b, a:a + 1])
                last.then_inc(h2_ready, 1)
            node_pairs(act, step)
            norm(PAIRS - 1, 0)

        @block.tensor
        def _(pe):
            def step(i, b, s, first):
                pe.wait_ge(relu_ready, i + 1)
                if not first:
                    pe.wait_ge(x2_ready, i - 1)
                pe.sem_inc(mark_pe, 1)
                for a in range(2):
                    for k in range(2):
                        last = nc.tensor.transpose(m.ps[b][:, D * a + P * k:D * a + P * (k + 1)],
                                                   relu[:, b, k, P * a:P * (a + 1)], m.ident[:, :])
                last.then_inc(turned, 1)
            node_pairs(pe, step)

        @block.vector
        def _(dve):
            nc.vector.tensor_tensor(m.coef[:, 0:SB, :, :], m.coef[:, 0:SB, :, :],
                                    m.radial.rearrange("p (t j) -> p t j", j=J).unsqueeze(3).to_broadcast([P, SB, J, 4]),
                                    ALU.mult).then_inc(scaled_coef, 1)
            dve.wait_ge(scaled_coef, 1)
            nc.vector.tensor_copy(m.coef[:, SB, :, :], m.coef[:, 0, :, :])

            def step(i, b, s, first):
                dve.wait_ge(xh_in[b], 16 * s + 16)
                dve.wait_ge(turned, i + 1)
                if not first:
                    dve.wait_ge(h2_ready, i - 1)
                    dve.wait_ge(out_s[b], 32 * s)
                nc.vector.tensor_tensor(x2[:, b], m.ps[b][:, :].rearrange("p (a f) -> p a f", a=2), xh[:, b],
                                        ALU.add).then_inc(x2_ready, 1)
                dve.wait_ge(x2_ready, i + 1)
                moments(nc, m, dve, chain, var_ready, std_ready, factors, mark_d, i, b, x2[:, b],
                        None if first else h2_ready)
            node_pairs(dve, step)

        @block.gpsimd
        def _(pool):
            def step(i, b, s, first):
                pool.wait_ge(x2_ready, i + 1)
                pool.sem_inc(mark_p, 1)
                pool.dma_start(pair_rows(m.x2_tab, i), x2[:, b]).then_inc(out_s[b], 16)
                pool.wait_ge(h2_ready, i + 1)
                pool.sem_inc(mark_p, 1)
                pool.dma_start(pair_rows(m.h2_tab, i), h2[:, b]).then_inc(out_s[b], 16)
            nc.gpsimd.memset(m.acc[:, 4, :], 0.0)
            nc.gpsimd.memset(m.acc[:, 2, :], 0.0)
            node_pairs(pool, step)
            pool.wait_ge(scaled_coef, 1)
            nc.gpsimd.memset(m.acc[:, 3, :], 0.0)
            pool.wait_ge(out_s[0], 32 * (PAIRS // 2 + 1))
            pool.wait_ge(out_s[1], 32 * (PAIRS // 2))


def output(nc, m, out):
    ctx = ExitStack()
    with ctx:
        x2_in = sems(nc, ctx, "o_x2_in0", "o_x2_in1")
        out_s = sems(nc, ctx, "o_out0", "o_out1")
        staged, mm_ready, y_ready, mark_a, mark_pe, mark_p = sems(
            nc, ctx, "o_staged", "o_mm", "o_y", "o_mark_a", "o_mark_pe", "o_mark_p")
        block = ctx.enter_context(nc.Block())
        stage = m.stage

        @block.sync
        def _(sp):
            def step(i, b, s, first):
                if not first:
                    sp.wait_ge(y_ready, i - 1)
                sp.dma_start(m.tile_in[:, b], pair_rows(m.x2_tab, i)).then_inc(x2_in[b], 16)
            node_pairs(sp, step)

        @block.scalar
        def _(act):
            def step(i, b, s, first):
                if not first:
                    act.wait_ge(mm_ready, i - 1)
                    act.sem_inc(mark_a, 1)
                nc.scalar.activation(stage[:, b], m.acc[:, :, bass.ds(i * (2 * P), 2 * P)], ACT.Copy).then_inc(staged, 1)
            node_pairs(act, step)

        @block.tensor
        def _(pe):
            def step(i, b, s, first):
                pe.wait_ge(staged, i + 1)
                if not first:
                    pe.wait_ge(y_ready, i - 1)
                pe.sem_inc(mark_pe, 1)
                for a in range(2):
                    for n, k in enumerate((2, 0, 1, 4, 3)):
                        c0, c1 = {0: (P, D), 1: (0, P), 4: (0, P)}.get(k, (0, D))
                        last = nc.tensor.matmul(m.ps[b][:, D * a + c0:D * a + c1], stage[:, b, k, P * a:P * (a + 1)],
                                                m.wk[:, k, c0:c1], start=(n == 0), stop=(n == 4))
                last.then_inc(mm_ready, 1)
            node_pairs(pe, step)

        @block.vector
        def _(dve):
            def step(i, b, s, first):
                dve.wait_ge(x2_in[b], 16 * s + 16)
                dve.wait_ge(mm_ready, i + 1)
                if not first:
                    dve.wait_ge(out_s[b], 16 * s)
                y = m.ps[b][:, :].rearrange("p (a f) -> p a f", a=2)
                nc.vector.tensor_tensor(m.tile_out[:, b, :, 0:MUL], m.tile_in[:, b, :, 0:MUL], y[:, :, 0:MUL], ALU.add)
                for a in range(2):
                    last = nc.vector.tensor_tensor(m.tile_out[:, b, a, MUL:D].rearrange("p (i v) -> p i v", v=3),
                                                   m.tile_in[:, b, a, MUL:D].rearrange("p (i v) -> p i v", v=3),
                                                   y[:, a, MUL:D].rearrange("p (v i) -> p i v", v=3), ALU.add)
                last.then_inc(y_ready, 1)
            node_pairs(dve, step)

        @block.gpsimd
        def _(pool):
            half = PAIRS // 2
            rest = N - (PAIRS - 1) * 2 * P

            def step(i, b, s, first):
                pool.wait_ge(y_ready, i + 1)
                pool.sem_inc(mark_p, 1)
                if isinstance(i, int) and i == PAIRS - 1:
                    assert rest <= P
                    pool.dma_start(out[i * 2 * P:N, :], m.tile_out[0:rest, b, 0, :]).then_inc(out_s[b], 16)
                else:
                    pool.dma_start(pair_rows(out, i), m.tile_out[:, b]).then_inc(out_s[b], 16)
            node_pairs(pool, step)
            pool.wait_ge(out_s[0], 16 * (half + 1))
            pool.wait_ge(out_s[1], 16 * half)


def build(nc, x, idx_rows, dst_rows, dst_slots, emb_rows, edge_attr_4, edge_weight, w1T, gamma1, beta1, w2T, eps,
          gamma_h, beta_h, w_00_0, w_11_0, w_01_1, w_10_1, fc_w1, fc_w2, out):
    ctx = ExitStack()
    with ctx:
        m = Memory(nc, ctx)
        constants(nc, m, dict(w1T=w1T, w2T=w2T, gamma1=gamma1, beta1=beta1, gamma_h=gamma_h, beta_h=beta_h, eps=eps,
                              w_00_0=w_00_0, w_11_0=w_11_0, w_01_1=w_01_1, w_10_1=w_10_1, fc_w1=fc_w1, fc_w2=fc_w2,
                              edge_weight=edge_weight, edge_attr_4=edge_attr_4, dst_slots=dst_slots))
        windows(nc, m, dst_rows)
        input_norm(nc, m, x)
        sweep(nc, m, 1, m.h_tab, idx_rows, emb_rows)
        product(nc, m, m.w1T, 1, 0, 1)
        product(nc, m, m.w2T, 2, 2, 3)
        between(nc, m)
        sweep(nc, m, 2, m.h2_tab, idx_rows, emb_rows)
        output(nc, m, out)


def kernel(x, src, dst, edge_attr_10, edge_attr_4, edge_weight, L0_gnn_w1, L0_gnn_gamma1, L0_gnn_beta1, L0_gnn_w2,
           L0_gnn_eps_weight, L0_gnn_gamma_h, L0_gnn_beta_h, L1_gnn_w_00_0, L1_gnn_w_11_0, L1_gnn_w_01_1,
           L1_gnn_w_10_1, L1_gnn_fc_w1, L1_gnn_fc_w2):
    import numpy as np
    import concourse.bacc as bacc
    from concourse.bass_utils import run_bass_kernel_spmd

    def superblocked(a, fill=0):
        a = np.asarray(a).reshape(E, -1)
        a = np.pad(a, ((0, SB * SB_EDGES - E), (0, 0)), constant_values=fill)
        return a.reshape(SB, P, J, -1)

    def by_partition(a):
        a = np.concatenate([a, a[:1]], axis=0)
        return np.ascontiguousarray(np.swapaxes(a, 0, 1).reshape(P, -1))

    def halves(v):
        return np.ascontiguousarray(np.asarray(v).reshape(2, P).T)

    dst4 = superblocked(dst, FAR)
    arrays = {
        "x": np.pad(np.asarray(x), ((0, NPAD - N), (0, 0))),
        "idx_rows": superblocked(src)[..., 0],
        "dst_rows": dst4.reshape(SB, SB_EDGES),
        "dst_slots": by_partition(dst4),
        "emb_rows": superblocked(edge_attr_10).transpose(0, 2, 3, 1).reshape(SB, J * EMB, P),
        "edge_attr_4": by_partition(superblocked(edge_attr_4)),
        "edge_weight": by_partition(superblocked(edge_weight)),
        "w1T": np.asarray(L0_gnn_w1).T, "gamma1": halves(L0_gnn_gamma1), "beta1": halves(L0_gnn_beta1),
        "w2T": np.asarray(L0_gnn_w2).T, "eps": np.asarray(L0_gnn_eps_weight).reshape(1, 1),
        "gamma_h": halves(L0_gnn_gamma_h), "beta_h": halves(L0_gnn_beta_h),
        "w_00_0": L1_gnn_w_00_0, "w_11_0": L1_gnn_w_11_0, "w_01_1": L1_gnn_w_01_1, "w_10_1": L1_gnn_w_10_1,
        "fc_w1": L1_gnn_fc_w1, "fc_w2": L1_gnn_fc_w2,
    }
    nc = bacc.Bacc("TRN2", target_bir_lowering=False, num_devices=1)
    given, args = {}, {}
    for name, a in arrays.items():
        a = np.ascontiguousarray(a)
        given[f"in_{name}"] = a
        args[name] = nc.dram_tensor(f"in_{name}", a.shape, mybir.dt.from_np(a.dtype), kind="ExternalInput").ap()
    out = nc.dram_tensor("out_y", (N, D), f32, kind="ExternalOutput").ap()
    build(nc, out=out, **args)
    r = run_bass_kernel_spmd(nc, [given], core_ids=[0])
    return r.results[0]["out_y"]
```

```python
import concourse.bass as bass
from concourse import mybir
from concourse.alu_op_type import AluOpType as ALU
from contextlib import ExitStack

N, E, D, MUL = 6250, 206250, 256, 64
P = 128
J = 4
SB_EDGES = P * J
SLOTS = 4
SB = -(-(-(-E // SB_EDGES)) // SLOTS) * SLOTS
STEPS = SB // SLOTS
W = 32
PAIRS = -(-N // (2 * P))
NPAD = PAIRS * 2 * P
FAR = 8192
CH = 400
NCH = NPAD // CH
LAST = N - (NCH - 1) * CH
EMB, HID = 10, 64
KROUND = 256
EPS = 1e-5
SILU_NORM = 1.679177
NEIGHBOURS = 16.0
DST_TILES = -(-SB // P)

f32, i32, bf16 = mybir.dt.float32, mybir.dt.int32, mybir.dt.bfloat16
ACT = mybir.ActivationFunctionType
AX = mybir.AxisListType


FEATURES = [MUL + 3 * i for i in range(MUL)] + list(range(MUL)) + [MUL + 3 * i + v for v in (1, 2) for i in range(MUL)]
PARTS = ((0, (2, 3)), (1, (0, 1)), (2, (1, 2)), (3, (3, 1)), (0, (0, 1)))
WK_BLOCKS = ((0, 0, 2, "w_10_1"), (0, 1, 3, "w_10_1"), (1, 0, 1, "w_11_0"), (1, 1, 0, "w_01_1"),
             (2, 0, 2, "w_01_1"), (2, 1, 1, "w_11_0"), (3, 0, 1, "w_11_0"), (3, 1, 3, "w_01_1"),
             (4, 0, 0, "w_10_1"), (4, 1, 1, "w_00_0"))


class Memory:

    def __init__(self, nc, ctx):
        def sb(name, shape, dt=f32):
            return ctx.enter_context(nc.sbuf_tensor(name, shape, dt))

        def dram(name, shape):
            return nc.dram_tensor(name, shape, f32).ap()

        self.big = sb("big", [P, 5 * NPAD])
        self.acc = self.big[:, :].rearrange("p (k n) -> p k n", k=5)
        self.agg3 = self.big[:, 0:3 * NPAD].rearrange("p (k n) -> p k n", k=3)
        self.deg = self.agg3[:, 2, :]
        at = [3 * NPAD]

        def part(n):
            at[0] += n
            assert at[0] <= 5 * NPAD
            return self.big[:, at[0] - n:at[0]]

        self.w_edge = part((SB + 1) * J)
        self.attr = part(SB * J * 4).rearrange("p (t j c) -> p t j c", j=J, c=4)
        self.w1T = part(2 * D).rearrange("p (k o) -> p k o", k=2)
        self.w2T = part(2 * D).rearrange("p (k o) -> p k o", k=2)
        self.emb = part(SLOTS * P).rearrange("p (u e) -> p u e", u=SLOTS)
        self.hid = part(2 * 2 * P).rearrange("p (b q e) -> p b q e", b=2, q=2)
        self.fc1 = part(4 * HID)
        self.sel0 = part(2 * J * W).rearrange("p (b j n) -> p b j n", b=2, j=J)
        self.agg_sb0 = part(2 * D).rearrange("p (b f) -> p b f", b=2)
        more = part(2 * 2 * D).rearrange("p (b t f) -> p b t f", b=2, t=2)
        self.rows = sb("rows", [P, SLOTS, J, D])
        self.idx = sb("idx", [P, SLOTS, J], i32)
        pair = self.rows[:, :, :, :].rearrange("p (a b) (c t) f -> p a b c t f", a=2, c=2)
        self.tile_in = pair[:, 0, 0]
        self.x_in = [self.tile_in[:, 0], self.tile_in[:, 1], more[:, 0], more[:, 1]]
        self.tile_mid = pair[:, 0, 1]
        self.tile_out = pair[:, 1, 0]
        self.tile_aux = pair[:, 1, 1]
        self.rel = sb("rel", [P, SB + 1, J])
        self.coef = sb("coef", [P, SB + 1, J, 4])
        self.sel = sb("sel", [P, 2, J, 4, W])
        self.stage = self.coef[:, 0:2 * 5 * 2 * P // (4 * J), :, :].rearrange("p (b x) j c -> p b (x j c)", b=2)\
            .rearrange("p b (k n) -> p b k n", k=5)
        def early(k):
            n = SB_EDGES // (4 * J)
            return self.coef[:, n * k:n * (k + 1), :, :].rearrange("p t j c -> p (t j c)")

        tiles = self.coef[:, 0:2 * DST_TILES * SB_EDGES // (4 * J), :, :].rearrange("p t j c -> p (t j c)")
        tiles = tiles.rearrange("p (z k e) -> p z k e", z=2, k=DST_TILES)
        self.dst_f, self.dst_z = tiles[:, 0], tiles[:, 1]
        self.diag_span, self.diag_min = early(2 * DST_TILES), early(2 * DST_TILES + 1)
        self.hT = self.sel[:, :, :, :, :].rearrange("p b j c n -> p b (j c n)")
        self.maskf = sb("maskf", [P, 2, J, W])
        self.maskb = sb("maskb", [P, 2, J, W], bf16)
        self.agg_sb = sb("agg_sb", [P, 2, D + MUL])
        self.base_bc = sb("base_bc", [P, DST_TILES * P])
        self.base_f = sb("base_f", [1, SB])
        self.base_i = sb("base_i", [1, SB], i32)
        self.rounds_i = sb("rounds_i", [1, 1], i32)
        self.iota0 = sb("iota0", [P, W])
        self.iota = sb("iota", [P, W])
        self.wk = sb("wk", [P, 5, D])
        self.fc2 = sb("fc2", [P, 2])
        self.ident = sb("ident", [P, P])
        self.ones = sb("ones", [P, P])
        self.ones_b = sb("ones_b", [P, P], bf16)
        self.bn_par = sb("bn_par", [P, 4, 2])
        self.eps_w = sb("eps_w", [P, 1])
        self.stats = sb("stats", [P, 2, NCH, 6])
        self.mv = sb("mv", [P, 2, 2])
        self.scale = sb("scale", [P, 2])
        self.shift = sb("shift", [P, 2])
        self.tmp2 = sb("tmp2", [P, 2])
        self.st6 = sb("st6", [P, 2, 2, 6])
        self.tmv = sb("tmv", [P, 2, 2, 2])
        self.rstd = sb("rstd", [P, 2, 2])
        self.nmr = sb("nmr", [P, 2, 2])
        self.std = sb("std", [P, 2, 2])
        self.eps_bn = sb("eps_bn", [P, 1])
        self.colmin = sb("colmin", [P, DST_TILES])
        self.colspan = sb("colspan", [P, DST_TILES])
        self.spanmax = sb("spanmax", [P, 1])
        self.thresh = sb("thresh", [P, KROUND])
        self.rounds_f = sb("rounds_f", [P, 1])

        self.ps = [ctx.enter_context(nc.psum_tensor(f"bank{i}", [P, 512], f32)) for i in range(8)]

        self.g_tab = dram("g_tab", [NPAD, D])
        self.xh_tab = dram("xh_tab", [NPAD, D])
        self.x2_tab = dram("x2_tab", [NPAD, D])
        self.h2_tab = dram("h2_tab", [NPAD, D])


def sems(nc, ctx, *names):
    return [ctx.enter_context(nc.semaphore(n)) for n in names]


def pair_rows(table, i):
    return table[bass.ds(i * (2 * P), 2 * P), :].rearrange("(a p) f -> p a f", p=P)


def at(i, *steps):
    return isinstance(i, int) and i in steps


def node_pairs(eng, step, peeled=2, unroll=2):
    assert PAIRS % unroll == 1 and peeled % unroll == 0
    for i in range(peeled):
        step(i, i % unroll, i // unroll, i < 2)
    with eng.Fori(peeled // unroll, PAIRS // unroll) as s:
        for b in range(unroll):
            step(unroll * s + b, b, s, False)
    step(PAIRS - 1, 0, PAIRS // unroll, False)


def moments(nc, m, dve, chain, var_ready, std_ready, ready, mark, i, b, src, factors_read):
    nc.vector.bn_stats(m.st6[:, b, 0, :], src[:, 0, :])
    nc.vector.bn_stats(m.st6[:, b, 1, :], src[:, 1, :]).then_inc(chain, 1)
    dve.wait_ge(chain, 2 * i + 1)
    dve.sem_inc(mark, 1)
    nc.vector.bn_aggr(m.tmv[:, b, 0, :], m.st6[:, b, 0, :])
    nc.vector.bn_aggr(m.tmv[:, b, 1, :], m.st6[:, b, 1, :]).then_inc(var_ready, 1)
    if factors_read is not None:
        dve.wait_ge(factors_read, i - 1)
    dve.wait_ge(std_ready, i + 1)
    nc.vector.reciprocal(m.rstd[:, b, :], m.std[:, b, :]).then_inc(chain, 1)
    dve.wait_ge(chain, 2 * i + 2)
    nc.vector.scalar_tensor_tensor(m.nmr[:, b, :], m.tmv[:, b, :, 0], -1.0, m.rstd[:, b, :],
                                   ALU.mult, ALU.mult).then_inc(ready, 1)


def root(nc, m, act, var_ready, std_ready, i, b):
    act.wait_ge(var_ready, i + 1)
    nc.scalar.activation(m.std[:, b, :], m.tmv[:, b, :, 1], ACT.Sqrt, bias=m.eps_bn[:, 0:1]).then_inc(std_ready, 1)


def prepare(nc, m, w, x, dst_rows):
    ctx = ExitStack()
    with ctx:
        x_in = sems(nc, ctx, *(f"n_x_in{b}" for b in range(4)))
        dst_in = sems(nc, ctx, *(f"n_dst_in{k}" for k in range(DST_TILES)))
        g_out = sems(nc, ctx, "n_g_out0", "n_g_out1")
        xh_out = sems(nc, ctx, "n_xh_out0", "n_xh_out1")
        (constants, small_in, early_in, table_in, made, col_ready, spread, chain, tail, var_ready, std_ready,
         factors, h_ready, xh_ready, hT_ready, hT_sb, g_ready, g_sb, gT_ready, addend, mark_a, mark_d, mark_pe,
         mark_p, mark_s) = sems(nc, ctx, *("n_" + n for n in (
             "constants", "small_in", "early_in", "table_in", "made", "col_ready", "spread",
             "chain", "tail", "var_ready", "std_ready", "factors", "h_ready", "xh_ready", "hT_ready", "hT_sb",
             "g_ready", "g_sb", "gT_ready", "addend", "mark_a", "mark_d", "mark_pe", "mark_p", "mark_s")))
        block = ctx.enter_context(nc.Block())
        hT_bank = [m.ps[b] for b in range(2)]
        g_bank = [m.ps[2 + b] for b in range(2)]
        gT_bank = [m.ps[4 + b] for b in range(2)]
        spans, bases = m.ps[6], m.ps[7]
        x_t, h_t, xh_t, g_t = m.x_in, m.tile_mid, m.tile_out, m.tile_aux
        half = PAIRS // 2
        alpha = (2.0 * MUL) ** -0.5

        @block.sync
        def _(sp):
            def store_g(i, b):
                sp.wait_ge(g_sb, i + 1)
                sp.sem_inc(mark_s, 1)
                sp.dma_start(pair_rows(m.g_tab, i), g_t[:, b]).then_inc(g_out[b], 16)

            def store_xh(i, b):
                sp.wait_ge(xh_ready, i + 1)
                sp.sem_inc(mark_s, 1)
                sp.dma_start(pair_rows(m.xh_tab, i), xh_t[:, b]).then_inc(xh_out[b], 16)

            def step(i, u, s, first):
                if not at(i, 0, 1, 2, 3):
                    sp.wait_ge(xh_ready, i - 3)
                sp.dma_start(x_t[u], pair_rows(x, i)).then_inc(x_in[u], 16)
                if not first:
                    store_xh(i - 2, u % 2)
                if not at(i, 0, 1, 2, 3):
                    store_g(i - 4, u % 2)
            node_pairs(sp, step, peeled=4, unroll=4)
            for i in range(PAIRS - 4, PAIRS):
                if i >= PAIRS - 2:
                    store_xh(i, i % 2)
                store_g(i, i % 2)
            for sem in (xh_out, g_out):
                sp.wait_ge(sem[0], 16 * (half + 1))
                sp.wait_ge(sem[1], 16 * half)

        @block.vector
        def _(dve):
            steps = [0]

            def link(ins):
                steps[0] += 1
                ins.then_inc(tail, 1)
                dve.wait_ge(tail, steps[0])

            def hT_out(i, b, first):
                dve.wait_ge(hT_ready, i + 1)
                if not first:
                    dve.wait_ge(g_ready, i - 1)
                nc.vector.tensor_copy(m.hT[:, b, :], hT_bank[b][:, :]).then_inc(hT_sb, 1)

            def step(i, u, s, first):
                b = u % 2
                dve.wait_ge(x_in[u], 16 * s + 16)
                moments(nc, m, dve, chain, var_ready, std_ready, factors, mark_d, i, b, x_t[u],
                        None if first else h_ready)
                if not at(i, 0):
                    hT_out(i - 1, 1 - b, first or at(i, 2))
                aside(i)

            def aside(i):
                for k in range(DST_TILES):
                    if at(i, k + 1):
                        dve.wait_ge(dst_in[k], 16)
                        link(nc.vector.tensor_copy(m.dst_f[:, k, :], m.dst_f[:, k, :].bitcast(i32)))
                    if at(i, k + 2):
                        link(nc.vector.scalar_tensor_tensor(m.dst_z[:, k, :], m.dst_f[:, k, :], float(FAR),
                                                            m.dst_f[:, k, :], ALU.is_lt, ALU.mult))
                        nc.vector.tensor_reduce(m.colmin[:, k:k + 1], m.dst_f[:, k, :], AX.X, ALU.min)
                    if at(i, k + 3):
                        link(nc.vector.tensor_reduce(m.colspan[:, k:k + 1], m.dst_z[:, k, :], AX.X, ALU.max))
                if at(i, DST_TILES + 3):
                    dve.wait_ge(constants, 3)
                    link(nc.vector.tensor_tensor(m.colspan[:, :], m.colspan[:, :], m.colmin[:, :], ALU.subtract))
                    for k in range(DST_TILES):
                        for diag, col in ((m.diag_span, m.colspan), (m.diag_min, m.colmin)):
                            last = nc.vector.tensor_scalar(diag[:, P * k:P * (k + 1)], m.ident[:, :], col[:, k:k + 1],
                                                           None, ALU.mult)
                    last.then_inc(col_ready, 1)
                if at(i, DST_TILES + 4):
                    dve.wait_ge(small_in, 16 * 5)
                    nc.vector.tensor_scalar_mul(m.fc2[:, :], m.fc2[:, :], SILU_NORM / HID ** 0.5 / NEIGHBOURS ** 0.5)
                    link(nc.vector.tensor_scalar_mul(m.wk[:, :, :], m.wk[:, :, :], alpha))
                    for k, part, column, name in WK_BLOCKS:
                        if name == "w_11_0":
                            block_of_k = m.wk[MUL * part:MUL * (part + 1), k, MUL * column:MUL * (column + 1)]
                            nc.vector.tensor_scalar_mul(block_of_k, block_of_k, 3.0 ** -0.5)
                if at(i, DST_TILES + 5):
                    dve.wait_ge(spread, 1)
                    dve.wait_ge(constants, 5)
                    link(nc.vector.tensor_scalar_min(m.base_bc[:, :], bases[:, 0:DST_TILES * P], float(NPAD - W)))
                    link(nc.vector.tensor_reduce(m.spanmax[:, :], spans[:, 0:DST_TILES * P], AX.X, ALU.max))
                if at(i, DST_TILES + 6):
                    link(nc.vector.tensor_scalar(m.thresh[:, :], m.thresh[:, :], m.spanmax[:, 0:1], None, ALU.is_le))
                    link(nc.vector.tensor_reduce(m.rounds_f[:, :], m.thresh[:, :], AX.X, ALU.add))
                    nc.vector.tensor_scalar_add(m.rounds_i[0:1, :], m.rounds_f[0:1, :], 1.0)
                    dve.wait_ge(table_in, 48)
                    rel = m.rel[:, :, :].rearrange("p t j -> p (t j)")
                    link(nc.vector.tensor_copy(rel, rel.bitcast(i32)))
                if at(i, DST_TILES + 7):
                    link(nc.vector.tensor_tensor(m.rel[:, 0:SB, :], m.rel[:, 0:SB, :],
                                                 m.base_bc[:, 0:SB].unsqueeze(2).to_broadcast([P, SB, J]), ALU.subtract))
                    nc.vector.tensor_scalar_add(m.rel[:, SB, :], m.rel[:, 0, :], -float(W))

            node_pairs(dve, step, peeled=12, unroll=4)
            hT_out(PAIRS - 1, 0, False)

        @block.scalar
        def _(act):
            act.dma_start(m.w1T, w["w1T"]).then_inc(early_in, 16)
            act.dma_start(m.eps_w[:, :], w["eps"].to_broadcast([P, 1])).then_inc(early_in, 16)
            act.wait_ge(constants, 1)
            for k in range(DST_TILES):
                rows = min(P, SB - P * k)
                act.dma_start(m.dst_f[0:rows, k, :].bitcast(i32), dst_rows[P * k:P * k + rows, :]).then_inc(dst_in[k], 16)
            act.dma_start(m.rel[:, :, :].rearrange("p t j -> p (t j)").bitcast(i32), w["dst_slots"]).then_inc(table_in, 16)
            act.dma_start(m.w_edge, w["edge_weight"]).then_inc(table_in, 16)
            act.dma_start(m.attr.rearrange("p t j c -> p (t j c)"), w["edge_attr_4"]).then_inc(table_in, 16)
            for to, name in ((m.w2T, "w2T"), (m.bn_par[:, :, :], "bn_par"), (m.wk[:, :, :], "wk"),
                             (m.fc1[0:J * EMB, :], "fc1"), (m.fc2[:, :], "fc2")):
                act.dma_start(to, w[name]).then_inc(small_in, 16)

            def g_evac(i, b, stored, first):
                act.wait_ge(g_ready, i + 1)
                if not first:
                    act.wait_ge(gT_ready, i - 1)
                    act.wait_ge(g_out[b], 16 * stored)
                nc.scalar.activation(g_t[:, b], g_bank[b][:, :].rearrange("p (a f) -> p a f", a=2), ACT.Copy).then_inc(g_sb, 1)

            def first_addend(i, b):
                act.wait_ge(gT_ready, i + 1)
                act.sem_inc(mark_a, 1)
                nc.scalar.activation(m.agg3[:, 0:2, bass.ds(i * (2 * P), 2 * P)],
                                     gT_bank[b][:, :].rearrange("p (k n) -> p k n", k=2), ACT.Copy,
                                     scale=m.eps_w[:, 0:1]).then_inc(addend, 1)

            def step(i, u, s, first):
                b = u % 2
                root(nc, m, act, var_ready, std_ready, i, b)
                act.wait_ge(factors, i + 1)
                if not first:
                    act.wait_ge(hT_ready, i - 1)
                    act.wait_ge(xh_ready, i - 1)
                for a in range(2):
                    last = nc.scalar.activation(h_t[:, b, a, :], x_t[u][:, a, :], ACT.Relu,
                                                bias=m.nmr[:, b, a:a + 1], scale=m.rstd[:, b, a:a + 1])
                last.then_inc(h_ready, 1)
                if not first:
                    g_evac(i - 2, b, 2 * s + u // 2 - 1, at(i, 2, 3))
                if not (first or at(i, 2)):
                    first_addend(i - 3, 1 - b)
            act.wait_ge(constants, 2)
            act.wait_ge(early_in, 32)
            node_pairs(act, step, peeled=4, unroll=4)
            g_evac(PAIRS - 2, 1, half - 1, False)
            first_addend(PAIRS - 3, 0)
            g_evac(PAIRS - 1, 0, half, False)
            first_addend(PAIRS - 2, 1)
            first_addend(PAIRS - 1, 0)

        @block.tensor
        def _(pe):
            def transpose_h(i, b, first):
                pe.wait_ge(h_ready, i + 1)
                if not first:
                    pe.wait_ge(hT_sb, i - 1)
                pe.sem_inc(mark_pe, 1)
                for a in range(2):
                    for k in range(2):
                        last = nc.tensor.transpose(hT_bank[b][:, 2 * P * k + P * a:2 * P * k + P * (a + 1)],
                                                   h_t[:, b, a, P * k:P * (k + 1)], m.ident[:, :])
                last.then_inc(hT_ready, 1)

            def multiply(i, b, first):
                pe.wait_ge(hT_sb, i + 1)
                if not first:
                    pe.wait_ge(g_sb, i - 1)
                pe.sem_inc(mark_pe, 1)
                for a in range(2):
                    for k in range(2):
                        last = nc.tensor.matmul(g_bank[b][:, D * a:D * (a + 1)],
                                                m.hT[:, b, 2 * P * k + P * a:2 * P * k + P * (a + 1)],
                                                m.w1T[:, k, :], start=(k == 0), stop=(k == 1))
                last.then_inc(g_ready, 1)

            def transpose_g(i, b, first):
                pe.wait_ge(g_sb, i + 1)
                if not first:
                    pe.wait_ge(addend, i - 1)
                pe.sem_inc(mark_pe, 1)
                for a in range(2):
                    for k in range(2):
                        last = nc.tensor.transpose(gT_bank[b][:, 2 * P * k + P * a:2 * P * k + P * (a + 1)],
                                                   g_t[:, b, a, P * k:P * (k + 1)], m.ident[:, :])
                last.then_inc(gT_ready, 1)

            def step(i, u, s, first):
                b = u % 2
                transpose_h(i, b, first)
                if not at(i, 0):
                    multiply(i - 1, 1 - b, first or at(i, 2))
                if not first:
                    transpose_g(i - 2, b, at(i, 2, 3))
                if at(i, DST_TILES + 3):
                    pe.wait_ge(col_ready, 1)
                    nc.tensor.matmul(spans[:, 0:DST_TILES * P], m.ones[:, :], m.diag_span, start=True, stop=True)
                    nc.tensor.matmul(bases[:, 0:DST_TILES * P], m.ones[:, :], m.diag_min, start=True, stop=True).then_inc(spread, 1)
            pe.wait_ge(constants, 4)
            pe.wait_ge(early_in, 32)
            node_pairs(pe, step, peeled=8, unroll=4)
            multiply(PAIRS - 1, 0, False)
            transpose_g(PAIRS - 2, 1, False)
            transpose_g(PAIRS - 1, 0, False)

        @block.gpsimd
        def _(pool):
            nc.gpsimd.memset(m.dst_f[:, DST_TILES - 1, :], 0.0).then_inc(constants, 1)
            nc.gpsimd.memset(m.eps_bn[:, :], EPS).then_inc(constants, 1)
            nc.gpsimd.memset(m.ident[:, :], 0.0).then_inc(made, 1)
            pool.wait_ge(made, 1)
            nc.gpsimd.affine_select(out=m.ident[:, :], in_=m.ident[:, :], compare_op=ALU.not_equal, fill=1.0,
                                    base=0, pattern=[[-1, P]], channel_multiplier=1).then_inc(constants, 1)
            nc.gpsimd.memset(m.ones[:, :], 1.0).then_inc(constants, 1)
            nc.gpsimd.iota(m.iota0[:, :], pattern=[[1, W]], base=0, channel_multiplier=0,
                           allow_small_or_imprecise_dtypes=True)
            nc.gpsimd.iota(m.thresh[:, :], pattern=[[W, KROUND]], base=W, channel_multiplier=0,
                           allow_small_or_imprecise_dtypes=True).then_inc(constants, 1)

            def step(i, u, s, first):
                b = u % 2
                pool.wait_ge(h_ready, i + 1)
                if not first:
                    pool.wait_ge(xh_out[b], 16 * (2 * s + u // 2))
                pool.sem_inc(mark_p, 1)
                nc.gpsimd.tensor_tensor(xh_t[:, b], x_t[u], h_t[:, b], ALU.add).then_inc(xh_ready, 1)
            node_pairs(pool, step, peeled=4, unroll=4)
            nc.gpsimd.memset(m.ones_b[:, :], 1.0)
            nc.gpsimd.memset(m.deg, 0.0)


def superblocks(nc, eng, m, body):
    rounds = eng.value_load(m.rounds_i[0:1, 0:1], min_val=1, max_val=KROUND)
    with eng.Fori(0, rounds) as r:
        with eng.Fori(0, STEPS) as i:
            for u in range(SLOTS):
                body(r * SB + i * SLOTS + u, i * SLOTS + u, u, r * STEPS + i)


def sweep(nc, m, layer, table, idx_rows, emb_rows):
    first = layer == 1
    tag = f"e{layer}_"
    ctx = ExitStack()
    with ctx:
        names = ("idx_landed", "emb_landed", "rows_landed")
        idx_landed, emb_landed, rows_landed = (sems(nc, ctx, *(f"{tag}{n}{u}" for u in range(SLOTS))) for n in names)
        (sel_ready, sums_ready, sums_sb, sumsT_ready, added, hid_ready, hid_sb, rad_ready, rad_sb, chain, mask_ready,
         mark_d, mark_pe, mark_p, mark_s) = sems(nc, ctx, *(tag + n for n in (
             "sel_ready", "sums_ready", "sums_sb", "sumsT_ready", "added", "hid_ready", "hid_sb", "rad_ready",
             "rad_sb", "chain", "mask_ready", "mark_d", "mark_pe", "mark_p", "mark_s")))
        block = ctx.enter_context(nc.Block())
        width = W if first else 4 * W
        sums = [m.ps[b][0:width, 0:D] for b in range(2)]
        sumsT = [m.ps[2 + b][:, 0:3 * W] for b in range(2)]
        hidden = [m.ps[4 + b][:, 0:2 * P] for b in range(2)]
        radial = [m.ps[6 + b][:, 0:J] for b in range(2)]
        sums_out = [(m.agg_sb0 if first else m.agg_sb)[0:width, b, :] for b in range(2)]
        accs = m.agg3 if first else m.acc

        @block.sync
        def _(sp):
            def step(g, t, u, n):
                sp.wait_ge(sums_sb, g + 1)
                sp.sem_inc(mark_s, 1)
                sp.dma_start(m.idx[:, u, :], idx_rows[bass.ds(t, 1), :, :].rearrange("t p j -> p (t j)")).then_inc(idx_landed[u], 16)
                if first:
                    sp.wait_ge(hid_sb, g + 1)
                    sp.sem_inc(mark_s, 1)
                    sp.dma_start(m.emb[0:J * EMB, u, :], emb_rows[bass.ds(t, 1), :, :].rearrange("t k e -> k (t e)")).then_inc(emb_landed[u], 16)
            superblocks(nc, sp, m, step)

        @block.gpsimd
        def _(pool):
            def step(g, t, u, n):
                pool.wait_ge(idx_landed[u], 16 * n + 16)
                pool.sem_inc(mark_p, 1)
                for j in range(J):
                    pool.indirect_dma_start(out=m.rows[:, u, j, :], out_offset=None, in_=table,
                                            in_offset=bass.IndirectOffsetOnAxis(ap=m.idx[:, u, j:j + 1], axis=0),
                                            bounds_check=N - 1, oob_is_err=False).then_inc(rows_landed[u], 16)
            superblocks(nc, pool, m, step)

        @block.tensor
        def _(pe):
            def step(g, t, u, n):
                b = u % 2
                if first:
                    pe.wait_ge(emb_landed[u], 16 * n + 16)
                    pe.wait_ge(hid_sb, g + SLOTS - 1)
                    pe.sem_inc(mark_pe, 1)
                    for q in range(2):
                        last = nc.tensor.matmul(hidden[b][:, P * q:P * (q + 1)], m.fc1[0:J * EMB, P * q:P * (q + 1)],
                                                m.emb[0:J * EMB, u, :], start=True, stop=True)
                    last.then_inc(hid_ready, 1)
                pe.wait_ge(rows_landed[u], 16 * J * (n + 1))
                pe.wait_ge(sel_ready, g + 1)
                pe.wait_ge(sums_sb, g + SLOTS - 1)
                pe.sem_inc(mark_pe, 1)
                for j in range(J):
                    sel = m.sel0[:, b, j, :] if first else m.sel[:, b, j, :, :].rearrange("p c n -> p (c n)")
                    last = nc.tensor.matmul(sums[b], sel, m.rows[:, u, j, :], start=(j == 0), stop=(j == J - 1))
                last.then_inc(sums_ready, 1)
                if first:
                    pe.wait_ge(hid_sb, g + SLOTS + 1)
                    pe.wait_ge(rad_sb, g + 1)
                    pe.sem_inc(mark_pe, 1)
                    for q in range(2):
                        last = nc.tensor.matmul(radial[b][:, 2 * q:2 * q + 2], m.hid[:, b, q, :], m.fc2[:, :],
                                                start=True, stop=True)
                    last.then_inc(rad_ready, 1)
                pe.wait_ge(added, g + 1)
                pe.sem_inc(mark_pe, 1)
                if first:
                    for j in range(J):
                        nc.tensor.matmul(sumsT[b][:, 2 * W:3 * W], m.ones_b[:, :], m.maskb[:, b, j, :],
                                         start=(j == 0), stop=(j == J - 1))
                pe.wait_ge(sums_sb, g + SLOTS + 1)
                pe.sem_inc(mark_pe, 1)
                if first:
                    for k in range(2):
                        last = nc.tensor.transpose(sumsT[b][:, W * k:W * (k + 1)], sums_out[b][:, P * k:P * (k + 1)],
                                                   m.ident[0:W, 0:W])
                else:
                    for q, (_, (col, _)) in enumerate(PARTS[:4]):
                        last = nc.tensor.transpose(m.ps[2 + b][:, P * q:P * (q + 1)],
                                                   sums_out[b][:, MUL * col:MUL * (col + 2)], m.ident[:, :])
                last.then_inc(sumsT_ready, 1)
            superblocks(nc, pe, m, step)

        @block.scalar
        def _(act):
            act.sem_inc(sums_sb, SLOTS)
            if first:
                act.sem_inc(hid_sb, SLOTS)

            def step(g, t, u, n):
                b = u % 2
                if first:
                    act.wait_ge(hid_ready, g + 1)
                    nc.scalar.activation(m.hid[:, b, :, :], hidden[b].rearrange("p (q e) -> p q e", q=2), ACT.Silu,
                                         scale=EMB ** -0.5).then_inc(hid_sb, 1)
                act.wait_ge(sums_ready, g + 1)
                if not first:
                    nc.scalar.activation(sums_out[b][:, D:D + MUL], sums[b][:, MUL:2 * MUL], ACT.Copy)
                nc.scalar.activation(sums_out[b][:, 0:D], sums[b], ACT.Copy).then_inc(sums_sb, 1)
            superblocks(nc, act, m, step)

        @block.vector
        def _(dve):
            dve.sem_inc(added, 2)
            dve.sem_inc(rad_sb, 2)

            def select(t, b, step, masks):
                mask = m.maskb[:, b] if first else m.maskf[:, b]
                rel = m.rel[:, bass.ds(t, 1), :].rearrange("p t j -> p (t j)")
                nc.vector.tensor_tensor(mask, m.iota[:, :].unsqueeze(1).to_broadcast([P, J, W]),
                                        rel.unsqueeze(2).to_broadcast([P, J, W]), ALU.is_equal).then_inc(mask_ready, 1)
                dve.wait_ge(mask_ready, masks + 1)
                if first:
                    w = m.w_edge[:, bass.ds(t * J, J)]
                    nc.vector.tensor_tensor(m.sel0[:, b], mask, w.unsqueeze(2).to_broadcast([P, J, W]),
                                            ALU.mult).then_inc(sel_ready, 1)
                else:
                    c = m.coef[:, bass.ds(t, 1), :, :].rearrange("p t j c -> p (t j) c")
                    nc.vector.tensor_tensor(m.sel[:, b], mask.unsqueeze(2).to_broadcast([P, J, 4, W]),
                                            c.unsqueeze(3).to_broadcast([P, J, 4, W]), ALU.mult).then_inc(sel_ready, 1)

            nc.vector.tensor_copy(m.iota[:, :], m.iota0[:, :])
            nc.vector.tensor_copy(m.base_f[:, :], m.base_bc[0:1, 0:SB])
            if not first:
                nc.vector.memset(m.acc[:, 0:2, :], 0.0)
            nc.vector.tensor_copy(m.base_i[:, :], m.base_bc[0:1, 0:SB]).then_inc(chain, 1)
            dve.wait_ge(chain, 1)
            select(0, 0, 0, 0)
            rounds = dve.value_load(m.rounds_i[0:1, 0:1], min_val=1, max_val=KROUND)
            with dve.Fori(0, rounds) as r:
                with dve.Fori(0, STEPS) as i:
                    for u in range(SLOTS):
                        g, t, b = r * SB + i * SLOTS + u, i * SLOTS + u, u % 2
                        base = dve.value_load(m.base_i[0:1, bass.ds(t, 1)], min_val=0, max_val=NPAD - W)
                        select(t + 1, 1 - b, g + 1, g + 1)
                        if first:
                            dve.wait_ge(rad_ready, g + 1)
                            dve.sem_inc(mark_d, 1)
                            nc.vector.tensor_tensor(m.coef[:, bass.ds(t, 1), :, :].rearrange("p t j c -> p (t j) c"),
                                                    m.attr[:, bass.ds(t, 1), :, :].rearrange("p t j c -> p (t j) c"),
                                                    radial[b].unsqueeze(2).to_broadcast([P, J, 4]), ALU.mult).then_inc(rad_sb, 1)
                        dve.wait_ge(added, g + 2)
                        dve.wait_ge(sumsT_ready, g + 1)
                        if first:
                            new = sumsT[b].rearrange("p (k n) -> p k n", n=W)
                        else:
                            new = bass.AP(tensor=m.ps[2 + b], offset=0, ap=[[512, P], [P + W, 4], [1, W]])
                            window = m.acc[:, 4, bass.ds(base, W)]
                            nc.vector.tensor_tensor(window, window, m.ps[2 + b][:, P:P + W], ALU.add)
                        window = accs[:, 0:3 if first else 4, bass.ds(base, W)]
                        nc.vector.tensor_tensor(window, window, new, ALU.add).then_inc(added, 1)
                dve.wait_ge(sel_ready, (r + 1) * SB + 1)
                nc.vector.tensor_scalar_add(m.iota[:, :], m.iota[:, :], float(W))
                nc.vector.tensor_scalar(m.base_f[:, :], m.base_f[:, :], float(W), float(NPAD - W),
                                        ALU.add, ALU.min).then_inc(chain, 1)
                dve.wait_ge(chain, 2 * r + 2)
                nc.vector.tensor_copy(m.base_i[:, :], m.base_f[:, :]).then_inc(chain, 1)
                dve.wait_ge(chain, 2 * r + 3)


def batch_factors(nc, m, dve, chain, at0, var_ready, std_ready, gamma, beta):
    for k in range(2):
        last = nc.vector.bn_aggr(m.mv[:, k, :], m.stats[:, k, :, :].rearrange("p c s -> p (c s)"))
    last.then_inc(var_ready, 1)
    dve.wait_ge(std_ready, 1)
    nc.vector.reciprocal(m.scale[:, :], m.tmp2[:, :]).then_inc(chain, 1)
    dve.wait_ge(chain, at0 + 1)
    nc.vector.tensor_tensor(m.scale[:, :], m.scale[:, :], m.bn_par[:, gamma, :], ALU.mult).then_inc(chain, 1)
    dve.wait_ge(chain, at0 + 2)
    nc.vector.tensor_tensor(m.tmp2[:, :], m.mv[:, :, 0], m.scale[:, :], ALU.mult).then_inc(chain, 1)
    dve.wait_ge(chain, at0 + 3)
    return nc.vector.tensor_tensor(m.shift[:, :], m.bn_par[:, beta, :], m.tmp2[:, :], ALU.subtract)


def second_product(nc, m):
    ctx = ExitStack()
    with ctx:
        (relu_ready, mm_ready, out_sb, stats_done, chain, deg_floor, deg_root, deg_ready, scale_ready, var1, std1,
         var2, std2, mark_d, mark_pe) = sems(nc, ctx, *("p_" + n for n in (
             "relu_ready", "mm_ready", "out_sb", "stats_done", "chain", "deg_floor", "deg_root", "deg_ready",
             "scale_ready", "var1", "std1", "var2", "std2", "mark_d", "mark_pe")))
        block = ctx.enter_context(nc.Block())
        banks = [[m.ps[2 * b + k][:, 0:CH] for k in range(2)] for b in range(2)]
        assert NCH % 2 == 0

        def chunks(eng, step):
            step(0, 0, True, CH)
            step(1, 1, True, CH)
            with eng.Fori(1, NCH // 2 - 1) as s:
                for b in range(2):
                    step(2 * s + b, b, False, CH)
            step(NCH - 2, 0, False, CH)
            step(NCH - 1, 1, False, LAST)

        @block.gpsimd
        def _(pool):
            nc.gpsimd.tensor_scalar(m.deg, m.deg, 1.0, None, ALU.max).then_inc(deg_floor, 1)

        @block.tensor
        def _(pe):
            def step(c, b, first, real):
                pe.wait_ge(relu_ready, c + 1)
                if not first:
                    pe.wait_ge(out_sb, c - 1)
                pe.sem_inc(mark_pe, 1)
                for k in range(2):
                    for q in range(2):
                        last = nc.tensor.matmul(banks[b][k], m.w2T[:, q, P * k:P * (k + 1)],
                                                m.agg3[:, q, bass.ds(c * CH, CH)], start=(q == 0), stop=(q == 1))
                last.then_inc(mm_ready, 1)
            chunks(pe, step)

        @block.scalar
        def _(act):
            act.wait_ge(deg_floor, 1)
            nc.scalar.activation(m.deg, m.deg, ACT.Sqrt).then_inc(deg_root, 1)
            act.wait_ge(var1, 1)
            nc.scalar.activation(m.tmp2[:, :], m.mv[:, :, 1], ACT.Sqrt, bias=m.eps_bn[:, 0:1]).then_inc(std1, 1)
            act.wait_ge(scale_ready, 1)

            def step(c, b, first, real):
                for k in range(2):
                    chunk = m.agg3[:, k, bass.ds(c * CH, CH)]
                    last = nc.scalar.activation(chunk, chunk, ACT.Relu, bias=m.shift[:, k:k + 1], scale=m.scale[:, k:k + 1])
                last.then_inc(relu_ready, 1)
            chunks(act, step)
            act.wait_ge(var2, 1)
            nc.scalar.activation(m.tmp2[:, :], m.mv[:, :, 1], ACT.Sqrt, bias=m.eps_bn[:, 0:1]).then_inc(std2, 1)

        @block.vector
        def _(dve):
            def statistics(c, real):
                for k in range(2):
                    last = nc.vector.bn_stats(m.stats[:, k, bass.ds(c, 1), :].rearrange("p c s -> p (c s)"),
                                              m.agg3[:, k, bass.ds(c * CH, real)])
                return last

            with dve.Fori(0, NCH - 1) as c:
                statistics(c, CH)
            statistics(NCH - 1, LAST).then_inc(stats_done, 1)
            dve.wait_ge(stats_done, 1)
            batch_factors(nc, m, dve, chain, 0, var1, std1, 0, 1).then_inc(scale_ready, 1)
            dve.wait_ge(deg_root, 1)
            nc.vector.reciprocal(m.deg, m.deg).then_inc(deg_ready, 1)
            dve.wait_ge(deg_ready, 1)

            def step(c, b, first, real):
                dve.wait_ge(mm_ready, c + 1)
                for k in range(2):
                    last = nc.vector.tensor_tensor(m.agg3[:, k, bass.ds(c * CH, CH)], banks[b][k],
                                                   m.deg[:, bass.ds(c * CH, CH)], ALU.mult)
                last.then_inc(out_sb, 1)
                dve.wait_ge(out_sb, c + 1)
                dve.sem_inc(mark_d, 1)
                last = statistics(c, real)
                if at(c, NCH - 1):
                    last.then_inc(stats_done, 1)
            chunks(dve, step)
            dve.wait_ge(stats_done, 2)
            batch_factors(nc, m, dve, chain, 3, var2, std2, 2, 3)


def between(nc, m):
    ctx = ExitStack()
    with ctx:
        xh_in = sems(nc, ctx, "b_xh_in0", "b_xh_in1")
        out_s = sems(nc, ctx, "b_out0", "b_out1")
        relu_ready, turned, x2_ready, var_ready, std_ready, factors, h2_ready, chain, mark_pe, mark_a, mark_d, mark_s = sems(
            nc, ctx, "b_relu", "b_turned", "b_x2", "b_var", "b_std", "b_factors", "b_h2", "b_chain", "b_mark_pe", "b_mark_a", "b_mark_d", "b_mark_s")
        block = ctx.enter_context(nc.Block())
        xh, relu, x2, h2 = m.tile_in, m.tile_mid, m.tile_out, m.tile_aux

        @block.sync
        def _(sp):
            def store(i, b):
                sp.wait_ge(x2_ready, i + 1)
                sp.sem_inc(mark_s, 1)
                sp.dma_start(pair_rows(m.x2_tab, i), x2[:, b]).then_inc(out_s[b], 16)
                sp.wait_ge(h2_ready, i + 1)
                sp.sem_inc(mark_s, 1)
                sp.dma_start(pair_rows(m.h2_tab, i), h2[:, b]).then_inc(out_s[b], 16)

            def step(i, b, s, first):
                if not first:
                    sp.wait_ge(x2_ready, i - 1)
                sp.dma_start(xh[:, b], pair_rows(m.xh_tab, i)).then_inc(xh_in[b], 16)
                if at(i, 1) or not first:
                    store(i - 1, 1 - b)
            node_pairs(sp, step)
            store(PAIRS - 1, 0)
            sp.wait_ge(out_s[0], 32 * (PAIRS // 2 + 1))
            sp.wait_ge(out_s[1], 32 * (PAIRS // 2))

        @block.scalar
        def _(act):
            def step(i, b, s, first):
                if not first:
                    act.wait_ge(turned, i - 1)
                    act.sem_inc(mark_a, 1)
                for k in range(2):
                    last = nc.scalar.activation(relu[:, b, k, :], m.agg3[:, k, bass.ds(i * (2 * P), 2 * P)], ACT.Relu,
                                                bias=m.shift[:, k:k + 1], scale=m.scale[:, k:k + 1])
                last.then_inc(relu_ready, 1)
                if not (first and i == 0):
                    norm(i - 1, 1 - b)

            def norm(i, b):
                root(nc, m, act, var_ready, std_ready, i, b)
                act.wait_ge(factors, i + 1)
                for a in range(2):
                    last = nc.scalar.activation(h2[:, b, a, :], x2[:, b, a, :], ACT.Relu,
                                                bias=m.nmr[:, b, a:a + 1], scale=m.rstd[:, b, a:a + 1])
                last.then_inc(h2_ready, 1)
            node_pairs(act, step)
            norm(PAIRS - 1, 0)

        @block.tensor
        def _(pe):
            def step(i, b, s, first):
                pe.wait_ge(relu_ready, i + 1)
                if not first:
                    pe.wait_ge(x2_ready, i - 1)
                pe.sem_inc(mark_pe, 1)
                for a in range(2):
                    for k in range(2):
                        last = nc.tensor.transpose(m.ps[b][:, D * a + P * k:D * a + P * (k + 1)],
                                                   relu[:, b, k, P * a:P * (a + 1)], m.ident[:, :])
                last.then_inc(turned, 1)
            node_pairs(pe, step)

        @block.vector
        def _(dve):
            nc.vector.tensor_copy(m.coef[:, SB, :, :], m.coef[:, 0, :, :])

            def step(i, b, s, first):
                dve.wait_ge(xh_in[b], 16 * s + 16)
                dve.wait_ge(turned, i + 1)
                if not first:
                    dve.wait_ge(h2_ready, i - 1)
                    dve.wait_ge(out_s[b], 32 * s)
                nc.vector.tensor_tensor(x2[:, b], m.ps[b][:, :].rearrange("p (a f) -> p a f", a=2), xh[:, b],
                                        ALU.add).then_inc(x2_ready, 1)
                dve.wait_ge(x2_ready, i + 1)
                moments(nc, m, dve, chain, var_ready, std_ready, factors, mark_d, i, b, x2[:, b],
                        None if first else h2_ready)
            node_pairs(dve, step)

        @block.gpsimd
        def _(pool):
            for k in range(2, 5):
                nc.gpsimd.memset(m.acc[:, k, :], 0.0)


def output(nc, m, out):
    ctx = ExitStack()
    with ctx:
        x2_in = sems(nc, ctx, "o_x2_in0", "o_x2_in1")
        out_s = sems(nc, ctx, "o_out0", "o_out1")
        staged, mm_ready, y_ready, mark_a, mark_pe, mark_p = sems(
            nc, ctx, "o_staged", "o_mm", "o_y", "o_mark_a", "o_mark_pe", "o_mark_p")
        block = ctx.enter_context(nc.Block())
        stage = m.stage

        @block.sync
        def _(sp):
            def step(i, b, s, first):
                if not first:
                    sp.wait_ge(y_ready, i - 1)
                sp.dma_start(m.tile_in[:, b], pair_rows(m.x2_tab, i)).then_inc(x2_in[b], 16)
            node_pairs(sp, step)

        @block.scalar
        def _(act):
            def step(i, b, s, first):
                if not first:
                    act.wait_ge(mm_ready, i - 1)
                    act.sem_inc(mark_a, 1)
                nc.scalar.activation(stage[:, b], m.acc[:, :, bass.ds(i * (2 * P), 2 * P)], ACT.Copy).then_inc(staged, 1)
            node_pairs(act, step)

        @block.tensor
        def _(pe):
            def step(i, b, s, first):
                pe.wait_ge(staged, i + 1)
                if not first:
                    pe.wait_ge(y_ready, i - 1)
                pe.sem_inc(mark_pe, 1)
                for a in range(2):
                    for n, (k, c0, c1) in enumerate(((1, 0, P), (0, P, D), (2, MUL, 3 * MUL), (3, MUL, D), (4, 0, P))):
                        last = nc.tensor.matmul(m.ps[b][:, D * a + c0:D * a + c1], stage[:, b, k, P * a:P * (a + 1)],
                                                m.wk[:, k, c0:c1], start=(n == 0), stop=(n == 4))
                last.then_inc(mm_ready, 1)
            node_pairs(pe, step)

        @block.vector
        def _(dve):
            def step(i, b, s, first):
                dve.wait_ge(x2_in[b], 16 * s + 16)
                dve.wait_ge(mm_ready, i + 1)
                if not first:
                    dve.wait_ge(out_s[b], 16 * s)
                nc.vector.tensor_tensor(m.tile_out[:, b], m.tile_in[:, b], m.ps[b][:, :].rearrange("p (a f) -> p a f", a=2),
                                        ALU.add).then_inc(y_ready, 1)
            node_pairs(dve, step)

        @block.gpsimd
        def _(pool):
            half = PAIRS // 2
            rest = N - (PAIRS - 1) * 2 * P

            def step(i, b, s, first):
                pool.wait_ge(y_ready, i + 1)
                pool.sem_inc(mark_p, 1)
                if isinstance(i, int) and i == PAIRS - 1:
                    assert rest <= P
                    pool.dma_start(out[i * 2 * P:N, :], m.tile_out[0:rest, b, 0, :]).then_inc(out_s[b], 16)
                else:
                    pool.dma_start(pair_rows(out, i), m.tile_out[:, b]).then_inc(out_s[b], 16)
            node_pairs(pool, step)
            pool.wait_ge(out_s[0], 16 * (half + 1))
            pool.wait_ge(out_s[1], 16 * half)


def build(nc, x, idx_rows, dst_rows, emb_rows, out, **w):
    ctx = ExitStack()
    with ctx:
        m = Memory(nc, ctx)
        prepare(nc, m, w, x, dst_rows)
        sweep(nc, m, 1, m.g_tab, idx_rows, emb_rows)
        second_product(nc, m)
        between(nc, m)
        sweep(nc, m, 2, m.h2_tab, idx_rows, emb_rows)
        output(nc, m, out)


def kernel(x, src, dst, edge_attr_10, edge_attr_4, edge_weight, L0_gnn_w1, L0_gnn_gamma1, L0_gnn_beta1, L0_gnn_w2,
           L0_gnn_eps_weight, L0_gnn_gamma_h, L0_gnn_beta_h, L1_gnn_w_00_0, L1_gnn_w_11_0, L1_gnn_w_01_1,
           L1_gnn_w_10_1, L1_gnn_fc_w1, L1_gnn_fc_w2):
    import numpy as np
    import concourse.bacc as bacc
    from concourse.bass_utils import run_bass_kernel_spmd

    def superblocked(a, fill=0):
        a = np.asarray(a).reshape(E, -1)
        a = np.pad(a, ((0, SB * SB_EDGES - E), (0, 0)), constant_values=fill)
        return a.reshape(SB, P, J, -1)

    def by_partition(a, again=True):
        if again:
            a = np.concatenate([a, a[:1]], axis=0)
        return np.swapaxes(a, 0, 1).reshape(P, -1)

    def halves(v):
        v = np.asarray(v)
        return np.swapaxes(v.reshape(2, P, -1), 0, 1)

    dst4 = superblocked(dst, FAR)
    fc1 = np.zeros((J * EMB, J * HID), np.float32)
    for j in range(J):
        fc1[EMB * j:EMB * (j + 1), HID * j:HID * (j + 1)] = L1_gnn_fc_w1
    fc2 = np.zeros((P, 2), np.float32)
    for j in range(2):
        fc2[HID * j:HID * (j + 1), j:j + 1] = L1_gnn_fc_w2
    weights = {"w_00_0": L1_gnn_w_00_0, "w_11_0": L1_gnn_w_11_0, "w_01_1": L1_gnn_w_01_1, "w_10_1": L1_gnn_w_10_1}
    wk = np.zeros((P, 5, D), np.float32)
    for k, part, column, name in WK_BLOCKS:
        wk[MUL * part:MUL * (part + 1), k, MUL * column:MUL * (column + 1)] = weights[name]
    arrays = {
        "x": np.pad(np.asarray(x)[:, FEATURES], ((0, NPAD - N), (0, 0))),
        "idx_rows": superblocked(src)[..., 0],
        "dst_rows": dst4.reshape(SB, SB_EDGES),
        "dst_slots": by_partition(dst4),
        "emb_rows": superblocked(edge_attr_10).transpose(0, 2, 3, 1).reshape(SB, J * EMB, P),
        "edge_attr_4": by_partition(superblocked(edge_attr_4), again=False),
        "edge_weight": by_partition(superblocked(edge_weight)),
        "w1T": halves(np.asarray(L0_gnn_w1).T[FEATURES, :]),
        "w2T": halves(np.asarray(L0_gnn_w2).T[:, FEATURES]),
        "bn_par": np.stack([halves(v)[..., 0] for v in (
            L0_gnn_gamma1, L0_gnn_beta1, np.asarray(L0_gnn_gamma_h)[FEATURES], np.asarray(L0_gnn_beta_h)[FEATURES])], axis=1),
        "eps": np.asarray(L0_gnn_eps_weight).reshape(1, 1),
        "fc1": fc1, "fc2": fc2, "wk": wk,
    }
    nc = bacc.Bacc("TRN2", target_bir_lowering=False, num_devices=1)
    given, args = {}, {}
    for name, a in arrays.items():
        a = np.ascontiguousarray(a)
        given[f"in_{name}"] = a
        args[name] = nc.dram_tensor(f"in_{name}", a.shape, mybir.dt.from_np(a.dtype), kind="ExternalInput").ap()
    out = nc.dram_tensor("out_y", (N, D), f32, kind="ExternalOutput").ap()
    build(nc, out=out, **args)
    r = run_bass_kernel_spmd(nc, [given], core_ids=[0])
    return np.ascontiguousarray(r.results[0]["out_y"][:, np.argsort(FEATURES)])
```

```python
import concourse.bass as bass
from concourse import mybir
from concourse.alu_op_type import AluOpType as ALU
from contextlib import ExitStack

N, E, D, MUL = 6250, 206250, 256, 64
P = 128
J = 4
SB_EDGES = P * J
SLOTS = 4
SB = -(-(-(-E // SB_EDGES)) // SLOTS) * SLOTS
REAL_SB = -(-E // SB_EDGES)
STEPS = SB // SLOTS
W = 32
PAIRS = -(-N // (2 * P))
NPAD = PAIRS * 2 * P
FAR = 8192
CH = 400
NCH = NPAD // CH
LAST = N - (NCH - 1) * CH
EMB, HID = 10, 64
XH_LOADS = 5
KROUND = 256
EPS = 1e-5
SILU_NORM = 1.679177
NEIGHBOURS = 16.0
DST_TILES = -(-SB // P)

f32, i32, bf16 = mybir.dt.float32, mybir.dt.int32, mybir.dt.bfloat16
ACT = mybir.ActivationFunctionType
AX = mybir.AxisListType


FEATURES = [MUL + 3 * i for i in range(MUL)] + list(range(MUL)) + [MUL + 3 * i + v for v in (1, 2) for i in range(MUL)]
PARTS = ((0, (2, 3)), (1, (0, 1)), (2, (1, 2)), (3, (3, 1)), (0, (0, 1)))
WK_BLOCKS = ((0, 0, 2, "w_10_1"), (0, 1, 3, "w_10_1"), (1, 0, 1, "w_11_0"), (1, 1, 0, "w_01_1"),
             (2, 0, 2, "w_01_1"), (2, 1, 1, "w_11_0"), (3, 0, 1, "w_11_0"), (3, 1, 3, "w_01_1"),
             (4, 0, 0, "w_10_1"), (4, 1, 1, "w_00_0"))


class Memory:

    def __init__(self, nc, ctx):
        def sb(name, shape, dt=f32):
            return ctx.enter_context(nc.sbuf_tensor(name, shape, dt))

        def dram(name, shape):
            return nc.dram_tensor(name, shape, f32).ap()

        self.big = sb("big", [P, 5 * NPAD])
        self.acc = self.big[:, :].rearrange("p (k n) -> p k n", k=5)
        self.agg3 = self.big[:, 0:3 * NPAD].rearrange("p (k n) -> p k n", k=3)
        self.deg = self.agg3[:, 2, :]
        at = [3 * NPAD]

        def part(n):
            at[0] += n
            assert at[0] <= 5 * NPAD
            return self.big[:, at[0] - n:at[0]]

        self.w_edge = part((SB + 1) * J)
        self.attr = part(SB * J * 4).rearrange("p (t j c) -> p t j c", j=J, c=4)
        self.w1T = part(2 * D).rearrange("p (k o) -> p k o", k=2)
        self.emb = part(SLOTS * P).rearrange("p (u e) -> p u e", u=SLOTS)
        self.hid = part(2 * 2 * P).rearrange("p (b q e) -> p b q e", b=2, q=2)
        self.fc1 = part(4 * HID)
        self.sel0 = part(2 * J * W).rearrange("p (b j n) -> p b j n", b=2, j=J)
        self.agg_sb0 = part(2 * D).rearrange("p (b f) -> p b f", b=2)
        more = part(2 * 2 * D).rearrange("p (b t f) -> p b t f", b=2, t=2)
        self.rows = sb("rows", [P, SLOTS, J, D])
        self.idx = sb("idx", [P, SLOTS, J], i32)
        tiles = self.rows[:, :, :, :].rearrange("p a (c t) f -> p (a c) t f", c=2)
        self.tile_a, self.tile_b = tiles[:, 0:4], tiles[:, 4:8]
        self.x_in = [self.tile_a[:, 0], self.tile_a[:, 1], more[:, 0], more[:, 1]]
        self.xh = self.big[:, 3 * NPAD:5 * NPAD].rearrange("p (t f) -> p t f", f=D)
        self.rel = sb("rel", [P, SB + 1, J])
        self.coef = sb("coef", [P, SB + 1, J, 4])
        self.sel = sb("sel", [P, 2, J, 4, W])
        self.stage = self.coef[:, 0:2 * 5 * 2 * P // (4 * J), :, :].rearrange("p (b x) j c -> p b (x j c)", b=2)\
            .rearrange("p b (k n) -> p b k n", k=5)

        def early(k):
            n = SB_EDGES // (4 * J)
            return self.coef[:, n * k:n * (k + 1), :, :].rearrange("p t j c -> p (t j c)")

        tiles = self.coef[:, 0:2 * DST_TILES * SB_EDGES // (4 * J), :, :].rearrange("p t j c -> p (t j c)")
        tiles = tiles.rearrange("p (z k e) -> p z k e", z=2, k=DST_TILES)
        self.dst_f, self.dst_z = tiles[:, 0], tiles[:, 1]
        self.diag_span, self.diag_min = early(2 * DST_TILES), early(2 * DST_TILES + 1)
        self.hT = self.sel[:, :, :, :, :].rearrange("p b j c n -> p b (j c n)")
        self.w2T = self.sel[:, 0, :, :, :].rearrange("p j c n -> p (j c n)").rearrange("p (k o) -> p k o", k=2)
        self.y = self.hT.rearrange("p b (k n) -> p b k n", k=2)
        self.maskf = sb("maskf", [P, 2, J, W])
        self.maskb = sb("maskb", [P, 2, J, W], bf16)
        self.agg_sb = sb("agg_sb", [P, 2, D + MUL])
        self.base_bc = sb("base_bc", [P, DST_TILES * P])
        self.base_f = sb("base_f", [1, SB])
        self.base_i = sb("base_i", [1, SB], i32)
        self.rounds_i = sb("rounds_i", [1, 1], i32)
        self.iota0 = sb("iota0", [P, W])
        self.iota = sb("iota", [P, W])
        self.wk = sb("wk", [P, 5, D])
        self.fc2 = sb("fc2", [P, 2])
        self.ident = sb("ident", [P, P])
        self.ones = sb("ones", [P, P])
        self.ones_b = sb("ones_b", [P, P], bf16)
        self.bn_par = sb("bn_par", [P, 4, 2])
        self.eps_w = sb("eps_w", [P, 1])
        self.stats = sb("stats", [P, 2, NCH, 6])
        self.mv = sb("mv", [P, 2, 2])
        self.scale = sb("scale", [P, 2])
        self.shift = sb("shift", [P, 2])
        self.tmp2 = sb("tmp2", [P, 2])
        self.st6 = sb("st6", [P, 4, 2, 6])
        self.tmv = sb("tmv", [P, 4, 2, 2])
        self.rstd = sb("rstd", [P, 4, 2])
        self.nmr = sb("nmr", [P, 4, 2])
        self.std = sb("std", [P, 4, 2])
        self.deg_nodes = sb("deg_nodes", [P, NPAD // P])
        self.eps_bn = sb("eps_bn", [P, 1])
        self.colmin = sb("colmin", [P, DST_TILES])
        self.colspan = sb("colspan", [P, DST_TILES])
        self.spanmax = sb("spanmax", [P, 1])
        self.thresh = sb("thresh", [P, KROUND])
        self.rounds_f = sb("rounds_f", [P, 1])

        self.ps = [ctx.enter_context(nc.psum_tensor(f"bank{i}", [P, 512], f32)) for i in range(8)]

        self.g_tab = dram("g_tab", [NPAD, D])
        self.xh_tab = dram("xh_tab", [NPAD, D])
        self.x2_tab = dram("x2_tab", [NPAD, D])
        self.h2_tab = dram("h2_tab", [NPAD, D])
        self.deg_row = dram("deg_row", [1, NPAD])
        self.norm_row = dram("norm_row", [1, NPAD])


def sems(nc, ctx, *names):
    return [ctx.enter_context(nc.semaphore(n)) for n in names]


def pair_rows(table, i):
    return table[bass.ds(i * (2 * P), 2 * P), :].rearrange("(a p) f -> p a f", p=P)


def tiles_of(i):
    assert P < 2 * P * PAIRS - N < 2 * P
    return 1 if at(i, PAIRS - 1) else 2


def at(i, *steps):
    return isinstance(i, int) and i in steps


def node_pairs(eng, step, peeled=2, unroll=2):
    assert PAIRS % unroll == 1 and peeled % unroll == 0
    for i in range(peeled):
        step(i, i % unroll, i // unroll, i < 2)
    with eng.Fori(peeled // unroll, PAIRS // unroll) as s:
        for b in range(unroll):
            step(unroll * s + b, b, s, False)
    step(PAIRS - 1, 0, PAIRS // unroll, False)


def variance(nc, m, dve, spread, var_ready, mark, i, b, src):
    nc.vector.bn_stats(m.st6[:, b, 0, :], src[:, 0, :])
    nc.vector.bn_stats(m.st6[:, b, 1, :], src[:, 1, :]).then_inc(spread, 1)
    dve.wait_ge(spread, i + 1)
    dve.sem_inc(mark, 1)
    nc.vector.bn_aggr(m.tmv[:, b, 0, :], m.st6[:, b, 0, :])
    nc.vector.bn_aggr(m.tmv[:, b, 1, :], m.st6[:, b, 1, :]).then_inc(var_ready, 1)


def norm_factors(nc, m, dve, inverse, std_ready, ready, i, b):
    dve.wait_ge(std_ready, i + 1)
    nc.vector.reciprocal(m.rstd[:, b, :], m.std[:, b, :]).then_inc(inverse, 1)
    dve.wait_ge(inverse, i + 1)
    nc.vector.scalar_tensor_tensor(m.nmr[:, b, :], m.tmv[:, b, :, 0], -1.0, m.rstd[:, b, :],
                                   ALU.mult, ALU.mult).then_inc(ready, 1)


def root(nc, m, act, var_ready, std_ready, i, b):
    act.wait_ge(var_ready, i + 1)
    nc.scalar.activation(m.std[:, b, :], m.tmv[:, b, :, 1], ACT.Sqrt, bias=m.eps_bn[:, 0:1]).then_inc(std_ready, 1)


def prepare(nc, m, w, x, idx_rows, dst_rows, emb_rows):
    ctx = ExitStack()
    with ctx:
        x_in = sems(nc, ctx, *(f"n_x_in{b}" for b in range(4)))
        dst_in = sems(nc, ctx, *(f"n_dst_in{k}" for k in range(DST_TILES)))
        g_out = sems(nc, ctx, "n_g_out0", "n_g_out1")
        xh_out = sems(nc, ctx, "n_xh_out0", "n_xh_out1")
        (constants, small_in, early_in, rel_in, table_in, made, col_ready, spread, moments, inverse, tail,
         var_ready, std_ready, factors, h_ready, xh_ready, hT_ready, hT_sb, g_ready, g_sb, gT_ready, addend, mark_a,
         mark_d, mark_pe, mark_p, mark_s) = sems(nc, ctx, *("n_" + n for n in (
             "constants", "small_in", "early_in", "rel_in", "table_in", "made", "col_ready", "spread",
             "moments", "inverse", "tail", "var_ready", "std_ready", "factors", "h_ready", "xh_ready", "hT_ready", "hT_sb",
             "g_ready", "g_sb", "gT_ready", "addend", "mark_a", "mark_d", "mark_pe", "mark_p", "mark_s")))
        block = ctx.enter_context(nc.Block())
        hT_bank = [m.ps[b] for b in range(2)]
        g_bank = [m.ps[2 + b] for b in range(2)]
        gT_bank = [m.ps[4 + b] for b in range(2)]
        spans, bases = m.ps[6], m.ps[7]
        x_t, h_t, xh_t, g_t = m.x_in, m.tile_a[:, 2:4], m.tile_b[:, 0:2], m.tile_b[:, 2:4]
        half = PAIRS // 2
        alpha = (2.0 * MUL) ** -0.5

        @block.sync
        def _(sp):
            def store_g(i, b):
                sp.wait_ge(g_sb, i + 1)
                sp.sem_inc(mark_s, 1)
                sp.dma_start(pair_rows(m.g_tab, i), g_t[:, b]).then_inc(g_out[b], 16)

            def store_xh(i, b):
                sp.wait_ge(xh_ready, i + 1)
                sp.sem_inc(mark_s, 1)
                sp.dma_start(pair_rows(m.xh_tab, i), xh_t[:, b]).then_inc(xh_out[b], 16)

            def tables(i):
                if at(i, 0):
                    sp.dma_start(m.w1T, w["w1T"]).then_inc(early_in, 16)
                    sp.dma_start(m.eps_w[:, :], w["eps"].to_broadcast([P, 1])).then_inc(early_in, 16)
                if at(i, 3):
                    sp.wait_ge(constants, 1)
                    for k in range(DST_TILES):
                        rows = min(P, SB - P * k)
                        sp.dma_start(m.dst_f[0:rows, k, :].bitcast(i32), dst_rows[P * k:P * k + rows, :]).then_inc(dst_in[k], 16)
                if at(i, 4):
                    sp.dma_start(m.rel[:, :, :].rearrange("p t j -> p (t j)").bitcast(i32), w["dst_slots"]).then_inc(rel_in, 16)
                if at(i, 5):
                    for to, name in ((m.bn_par[:, :, :], "bn_par"), (m.wk[:, :, :], "wk"), (m.fc1[0:J * EMB, :], "fc1"),
                                     (m.fc2[:, :], "fc2")):
                        sp.dma_start(to, w[name]).then_inc(small_in, 16)
                if at(i, 6):
                    sp.dma_start(m.w_edge, w["edge_weight"]).then_inc(table_in, 16)
                    sp.dma_start(m.idx[:, :, :], idx_rows[0:SLOTS, :, :].rearrange("t p j -> p t j")).then_inc(table_in, 16)
                    sp.dma_start(m.emb[0:J * EMB, :, :], emb_rows[0:SLOTS, :, :].rearrange("t k e -> k t e")).then_inc(table_in, 16)
                for k in range(4):
                    if at(i, 8 + k):
                        n = SB // 4
                        sp.dma_start(m.attr[:, n * k:n * (k + 1)].rearrange("p t j c -> p (t j c)"),
                                     w["edge_attr_4"][:, n * k * 4 * J:n * (k + 1) * 4 * J]).then_inc(table_in, 16)

            def step(i, u, s, first):
                if not at(i, 0, 1, 2, 3):
                    sp.wait_ge(xh_ready, i - 3)
                sp.dma_start(x_t[u], pair_rows(x, i)).then_inc(x_in[u], 16)
                tables(i)
                if not first:
                    store_xh(i - 2, u % 2)
                if not at(i, 0, 1, 2, 3):
                    store_g(i - 4, u % 2)
            node_pairs(sp, step, peeled=12, unroll=4)
            sp.wait_ge(table_in, 16 * 7)
            for i in range(PAIRS - 4, PAIRS):
                if i >= PAIRS - 2:
                    store_xh(i, i % 2)
                store_g(i, i % 2)
            for sem in (xh_out, g_out):
                sp.wait_ge(sem[0], 16 * (half + 1))
                sp.wait_ge(sem[1], 16 * half)

        @block.vector
        def _(dve):
            steps = [0]

            def link(ins):
                steps[0] += 1
                ins.then_inc(tail, 1)
                dve.wait_ge(tail, steps[0])

            def hT_out(i, b, first):
                dve.wait_ge(hT_ready, i + 1)
                if not first:
                    dve.wait_ge(g_ready, i - 1)
                nc.vector.tensor_copy(m.hT[:, b, :], hT_bank[b][:, :]).then_inc(hT_sb, 1)

            def step(i, u, s, first):
                b = u % 2
                dve.wait_ge(x_in[u], 16 * s + 16)
                variance(nc, m, dve, moments, var_ready, mark_d, i, b, x_t[u])
                if not first:
                    dve.wait_ge(h_ready, i - 1)
                norm_factors(nc, m, dve, inverse, std_ready, factors, i, b)
                if not at(i, 0):
                    hT_out(i - 1, 1 - b, first or at(i, 2))
                aside(i)

            def aside(i):
                for k in range(DST_TILES):
                    if at(i, k + 1):
                        dve.wait_ge(dst_in[k], 16)
                        link(nc.vector.tensor_copy(m.dst_f[:, k, :], m.dst_f[:, k, :].bitcast(i32)))
                    if at(i, k + 2):
                        link(nc.vector.scalar_tensor_tensor(m.dst_z[:, k, :], m.dst_f[:, k, :], float(FAR),
                                                            m.dst_f[:, k, :], ALU.is_lt, ALU.mult))
                        nc.vector.tensor_reduce(m.colmin[:, k:k + 1], m.dst_f[:, k, :], AX.X, ALU.min)
                    if at(i, k + 3):
                        link(nc.vector.tensor_reduce(m.colspan[:, k:k + 1], m.dst_z[:, k, :], AX.X, ALU.max))
                if at(i, DST_TILES + 3):
                    dve.wait_ge(constants, 3)
                    link(nc.vector.tensor_tensor(m.colspan[:, :], m.colspan[:, :], m.colmin[:, :], ALU.subtract))
                    for k in range(DST_TILES):
                        for diag, col in ((m.diag_span, m.colspan), (m.diag_min, m.colmin)):
                            last = nc.vector.tensor_scalar(diag[:, P * k:P * (k + 1)], m.ident[:, :], col[:, k:k + 1],
                                                           None, ALU.mult)
                    last.then_inc(col_ready, 1)
                if at(i, DST_TILES + 4):
                    dve.wait_ge(small_in, 16 * 4)
                    nc.vector.tensor_scalar_mul(m.fc2[:, :], m.fc2[:, :], SILU_NORM / HID ** 0.5 / NEIGHBOURS ** 0.5)
                    link(nc.vector.tensor_scalar_mul(m.wk[:, :, :], m.wk[:, :, :], alpha))
                    for k, part, column, name in WK_BLOCKS:
                        if name == "w_11_0":
                            block_of_k = m.wk[MUL * part:MUL * (part + 1), k, MUL * column:MUL * (column + 1)]
                            nc.vector.tensor_scalar_mul(block_of_k, block_of_k, 3.0 ** -0.5)
                if at(i, DST_TILES + 5):
                    dve.wait_ge(spread, 1)
                    dve.wait_ge(constants, 5)
                    link(nc.vector.tensor_scalar_min(m.base_bc[:, :], bases[:, 0:DST_TILES * P], float(NPAD - W)))
                    link(nc.vector.tensor_reduce(m.spanmax[:, :], spans[:, 0:DST_TILES * P], AX.X, ALU.max))
                if at(i, DST_TILES + 6):
                    link(nc.vector.tensor_scalar(m.thresh[:, :], m.thresh[:, :], m.spanmax[:, 0:1], None, ALU.is_le))
                    link(nc.vector.tensor_reduce(m.rounds_f[:, :], m.thresh[:, :], AX.X, ALU.add))
                    nc.vector.tensor_scalar_add(m.rounds_i[0:1, :], m.rounds_f[0:1, :], 1.0)
                    dve.wait_ge(rel_in, 16)
                    rel = m.rel[:, :, :].rearrange("p t j -> p (t j)")
                    link(nc.vector.tensor_copy(rel, rel.bitcast(i32)))
                if at(i, DST_TILES + 7):
                    link(nc.vector.tensor_tensor(m.rel[:, 0:SB, :], m.rel[:, 0:SB, :],
                                                 m.base_bc[:, 0:SB].unsqueeze(2).to_broadcast([P, SB, J]), ALU.subtract))
                    nc.vector.tensor_scalar_add(m.rel[:, SB, :], m.rel[:, 0, :], -float(W))

            node_pairs(dve, step, peeled=12, unroll=4)
            hT_out(PAIRS - 1, 0, False)

        @block.scalar
        def _(act):
            def g_evac(i, b, stored, first):
                act.wait_ge(g_ready, i + 1)
                if not first:
                    act.wait_ge(gT_ready, i - 1)
                    act.wait_ge(g_out[b], 16 * stored)
                nc.scalar.activation(g_t[:, b], g_bank[b][:, :].rearrange("p (a f) -> p a f", a=2), ACT.Copy).then_inc(g_sb, 1)

            def first_addend(i, b):
                act.wait_ge(gT_ready, i + 1)
                act.sem_inc(mark_a, 1)
                nc.scalar.activation(m.agg3[:, 0:2, bass.ds(i * (2 * P), 2 * P)],
                                     gT_bank[b][:, :].rearrange("p (k n) -> p k n", k=2), ACT.Copy,
                                     scale=m.eps_w[:, 0:1]).then_inc(addend, 1)

            def step(i, u, s, first):
                b = u % 2
                root(nc, m, act, var_ready, std_ready, i, b)
                act.wait_ge(factors, i + 1)
                if not first:
                    act.wait_ge(hT_ready, i - 1)
                    act.wait_ge(xh_ready, i - 1)
                for a in range(2):
                    last = nc.scalar.activation(h_t[:, b, a, :], x_t[u][:, a, :], ACT.Relu,
                                                bias=m.nmr[:, b, a:a + 1], scale=m.rstd[:, b, a:a + 1])
                last.then_inc(h_ready, 1)
                if not first:
                    g_evac(i - 2, b, 2 * s + u // 2 - 1, at(i, 2, 3))
                if not (first or at(i, 2)):
                    first_addend(i - 3, 1 - b)
            act.wait_ge(constants, 2)
            act.wait_ge(early_in, 32)
            node_pairs(act, step, peeled=4, unroll=4)
            g_evac(PAIRS - 2, 1, half - 1, False)
            first_addend(PAIRS - 3, 0)
            g_evac(PAIRS - 1, 0, half, False)
            first_addend(PAIRS - 2, 1)
            first_addend(PAIRS - 1, 0)

        @block.tensor
        def _(pe):
            def transpose_h(i, b, first):
                pe.wait_ge(h_ready, i + 1)
                if not first:
                    pe.wait_ge(hT_sb, i - 1)
                pe.sem_inc(mark_pe, 1)
                for a in range(tiles_of(i)):
                    for k in range(2):
                        last = nc.tensor.transpose(hT_bank[b][:, 2 * P * k + P * a:2 * P * k + P * (a + 1)],
                                                   h_t[:, b, a, P * k:P * (k + 1)], m.ident[:, :])
                last.then_inc(hT_ready, 1)

            def multiply(i, b, first):
                pe.wait_ge(hT_sb, i + 1)
                if not first:
                    pe.wait_ge(g_sb, i - 1)
                pe.sem_inc(mark_pe, 1)
                for a in range(tiles_of(i)):
                    for k in range(2):
                        last = nc.tensor.matmul(g_bank[b][:, D * a:D * (a + 1)],
                                                m.hT[:, b, 2 * P * k + P * a:2 * P * k + P * (a + 1)],
                                                m.w1T[:, k, :], start=(k == 0), stop=(k == 1))
                last.then_inc(g_ready, 1)

            def transpose_g(i, b, first):
                pe.wait_ge(g_sb, i + 1)
                if not first:
                    pe.wait_ge(addend, i - 1)
                pe.sem_inc(mark_pe, 1)
                for a in range(tiles_of(i)):
                    for k in range(2):
                        last = nc.tensor.transpose(gT_bank[b][:, 2 * P * k + P * a:2 * P * k + P * (a + 1)],
                                                   g_t[:, b, a, P * k:P * (k + 1)], m.ident[:, :])
                last.then_inc(gT_ready, 1)

            def step(i, u, s, first):
                b = u % 2
                transpose_h(i, b, first)
                if not at(i, 0):
                    multiply(i - 1, 1 - b, first or at(i, 2))
                if not first:
                    transpose_g(i - 2, b, at(i, 2, 3))
                if at(i, DST_TILES + 3):
                    pe.wait_ge(col_ready, 1)
                    nc.tensor.matmul(spans[:, 0:DST_TILES * P], m.ones[:, :], m.diag_span, start=True, stop=True)
                    nc.tensor.matmul(bases[:, 0:DST_TILES * P], m.ones[:, :], m.diag_min, start=True, stop=True).then_inc(spread, 1)
            pe.wait_ge(constants, 4)
            pe.wait_ge(early_in, 32)
            node_pairs(pe, step, peeled=8, unroll=4)
            multiply(PAIRS - 1, 0, False)
            transpose_g(PAIRS - 2, 1, False)
            transpose_g(PAIRS - 1, 0, False)

        @block.gpsimd
        def _(pool):
            nc.gpsimd.memset(m.dst_f[:, DST_TILES - 1, :], 0.0).then_inc(constants, 1)
            nc.gpsimd.memset(m.eps_bn[:, :], EPS).then_inc(constants, 1)
            nc.gpsimd.memset(m.ident[:, :], 0.0).then_inc(made, 1)
            pool.wait_ge(made, 1)
            nc.gpsimd.affine_select(out=m.ident[:, :], in_=m.ident[:, :], compare_op=ALU.not_equal, fill=1.0,
                                    base=0, pattern=[[-1, P]], channel_multiplier=1).then_inc(constants, 1)
            nc.gpsimd.memset(m.ones[:, :], 1.0).then_inc(constants, 1)
            nc.gpsimd.iota(m.iota0[:, :], pattern=[[1, W]], base=0, channel_multiplier=0,
                           allow_small_or_imprecise_dtypes=True)
            nc.gpsimd.iota(m.thresh[:, :], pattern=[[W, KROUND]], base=W, channel_multiplier=0,
                           allow_small_or_imprecise_dtypes=True).then_inc(constants, 1)

            def step(i, u, s, first):
                b = u % 2
                pool.wait_ge(h_ready, i + 1)
                if not first:
                    pool.wait_ge(xh_out[b], 16 * (2 * s + u // 2))
                pool.sem_inc(mark_p, 1)
                nc.gpsimd.tensor_tensor(xh_t[:, b], x_t[u], h_t[:, b], ALU.add).then_inc(xh_ready, 1)
            node_pairs(pool, step, peeled=4, unroll=4)
            nc.gpsimd.memset(m.ones_b[:, :], 1.0)
            nc.gpsimd.memset(m.deg, 0.0)


def superblocks(nc, eng, m, body, peel_last=False):
    rounds = eng.value_load(m.rounds_i[0:1, 0:1], min_val=1, max_val=KROUND)
    with eng.Fori(0, rounds) as r:
        def step(i, u):
            unfilled = REAL_SB <= SB - SLOTS + u
            body(r * SB + i * SLOTS + u, i * SLOTS + u, u, r * STEPS + i, r * (STEPS - unfilled) + i)
        with eng.Fori(0, STEPS - peel_last) as i:
            for u in range(SLOTS):
                step(i, u)
        if peel_last:
            for u in range(SLOTS):
                step(STEPS - 1, u)


def sweep(nc, m, layer, table, idx_rows, emb_rows):
    first = layer == 1
    tag = f"e{layer}_"
    ctx = ExitStack()
    with ctx:
        names = ("idx_landed", "emb_landed", "rows_landed")
        idx_landed, emb_landed, rows_landed = (sems(nc, ctx, *(f"{tag}{n}{u}" for u in range(SLOTS))) for n in names)
        (sel_ready, sums_ready, sums_sb, sumsT_ready, added, hid_ready, hid_sb, rad_ready, rad_sb, chain, mask_ready,
         mark_d, mark_pe, mark_p, mark_s) = sems(nc, ctx, *(tag + n for n in (
             "sel_ready", "sums_ready", "sums_sb", "sumsT_ready", "added", "hid_ready", "hid_sb", "rad_ready",
             "rad_sb", "chain", "mask_ready", "mark_d", "mark_pe", "mark_p", "mark_s")))
        block = ctx.enter_context(nc.Block())
        width = W if first else 4 * W
        sums = [m.ps[b][0:width, 0:D] for b in range(2)]
        sumsT = [m.ps[2 + b][:, 0:3 * W] for b in range(2)]
        hidden = [m.ps[4 + b][:, 0:2 * P] for b in range(2)]
        radial = [m.ps[6 + b][:, 0:J] for b in range(2)]
        sums_out = [(m.agg_sb0 if first else m.agg_sb)[0:width, b, :] for b in range(2)]
        accs = m.agg3 if first else m.acc
        padding = range(REAL_SB, SB)

        @block.sync
        def _(sp):
            for u in range(SLOTS):
                sp.sem_inc(idx_landed[u], 16)
                if first:
                    sp.sem_inc(emb_landed[u], 16)

            def step(g, t, u, n, f):
                if first:
                    sp.wait_ge(hid_sb, g + 1 + SLOTS)
                    sp.sem_inc(mark_s, 1)
                    sp.dma_start(m.emb[0:J * EMB, u, :], emb_rows[bass.ds(t + SLOTS, 1), :, :].rearrange("t k e -> k (t e)")).then_inc(emb_landed[u], 16)
                sp.wait_ge(sums_sb, g + 1 + SLOTS)
                sp.sem_inc(mark_s, 1)
                sp.dma_start(m.idx[:, u, :], idx_rows[bass.ds(t + SLOTS, 1), :, :].rearrange("t p j -> p (t j)")).then_inc(idx_landed[u], 16)
            superblocks(nc, sp, m, step)
            rounds = sp.value_load(m.rounds_i[0:1, 0:1], min_val=1, max_val=KROUND)
            for u in range(SLOTS):
                for landed in (idx_landed, emb_landed)[:1 + first]:
                    sp.wait_ge(landed[u], rounds * (16 * STEPS) + 16)
                    sp.sem_inc(mark_s, 1)

        @block.gpsimd
        def _(pool):
            def step(g, t, u, n, f):
                if at(t, *padding):
                    return
                pool.wait_ge(idx_landed[u], 16 * n + 16)
                pool.sem_inc(mark_p, 1)
                for j in range(J):
                    pool.indirect_dma_start(out=m.rows[:, u, j, :], out_offset=None, in_=table,
                                            in_offset=bass.IndirectOffsetOnAxis(ap=m.idx[:, u, j:j + 1], axis=0),
                                            bounds_check=N - 1, oob_is_err=False).then_inc(rows_landed[u], 16)
            superblocks(nc, pool, m, step, peel_last=True)

        @block.tensor
        def _(pe):
            def step(g, t, u, n, f):
                b = u % 2
                if first:
                    pe.wait_ge(emb_landed[u], 16 * n + 16)
                    pe.wait_ge(hid_sb, g + SLOTS - 1)
                    pe.sem_inc(mark_pe, 1)
                    for q in range(2):
                        last = nc.tensor.matmul(hidden[b][:, P * q:P * (q + 1)], m.fc1[0:J * EMB, P * q:P * (q + 1)],
                                                m.emb[0:J * EMB, u, :], start=True, stop=True)
                    last.then_inc(hid_ready, 1)
                if at(t, *padding):
                    pe.wait_ge(idx_landed[u], 16 * n + 16)
                    pe.sem_inc(mark_pe, 1)
                else:
                    pe.wait_ge(rows_landed[u], 16 * J * (f + 1))
                pe.wait_ge(sel_ready, g + 1)
                pe.wait_ge(sums_sb, g + SLOTS - 1)
                pe.sem_inc(mark_pe, 1)
                for j in range(J):
                    sel = m.sel0[:, b, j, :] if first else m.sel[:, b, j, :, :].rearrange("p c n -> p (c n)")
                    last = nc.tensor.matmul(sums[b], sel, m.rows[:, u, j, :], start=(j == 0), stop=(j == J - 1))
                last.then_inc(sums_ready, 1)
                if first:
                    pe.wait_ge(hid_sb, g + SLOTS + 1)
                    pe.wait_ge(rad_sb, g + 1)
                    pe.sem_inc(mark_pe, 1)
                    for q in range(2):
                        last = nc.tensor.matmul(radial[b][:, 2 * q:2 * q + 2], m.hid[:, b, q, :], m.fc2[:, :],
                                                start=True, stop=True)
                    last.then_inc(rad_ready, 1)
                pe.wait_ge(added, g + 1)
                pe.sem_inc(mark_pe, 1)
                if first:
                    for j in range(J):
                        nc.tensor.matmul(sumsT[b][:, 2 * W:3 * W], m.ones_b[:, :], m.maskb[:, b, j, :],
                                         start=(j == 0), stop=(j == J - 1))
                pe.wait_ge(sums_sb, g + SLOTS + 1)
                pe.sem_inc(mark_pe, 1)
                if first:
                    for k in range(2):
                        last = nc.tensor.transpose(sumsT[b][:, W * k:W * (k + 1)], sums_out[b][:, P * k:P * (k + 1)],
                                                   m.ident[0:W, 0:W])
                else:
                    for q, (_, (col, _)) in enumerate(PARTS[:4]):
                        last = nc.tensor.transpose(m.ps[2 + b][:, P * q:P * (q + 1)],
                                                   sums_out[b][:, MUL * col:MUL * (col + 2)], m.ident[:, :])
                last.then_inc(sumsT_ready, 1)
            superblocks(nc, pe, m, step, peel_last=True)

        @block.scalar
        def _(act):
            act.sem_inc(sums_sb, SLOTS)
            if first:
                act.sem_inc(hid_sb, SLOTS)

            def step(g, t, u, n, f):
                b = u % 2
                if first:
                    act.wait_ge(hid_ready, g + 1)
                    nc.scalar.activation(m.hid[:, b, :, :], hidden[b].rearrange("p (q e) -> p q e", q=2), ACT.Silu,
                                         scale=EMB ** -0.5).then_inc(hid_sb, 1)
                act.wait_ge(sums_ready, g + 1)
                if not first:
                    nc.scalar.activation(sums_out[b][:, D:D + MUL], sums[b][:, MUL:2 * MUL], ACT.Copy)
                nc.scalar.activation(sums_out[b][:, 0:D], sums[b], ACT.Copy).then_inc(sums_sb, 1)
            superblocks(nc, act, m, step)

        @block.vector
        def _(dve):
            dve.sem_inc(added, 2)
            dve.sem_inc(rad_sb, 2)

            def select(t, b, step, masks):
                mask = m.maskb[:, b] if first else m.maskf[:, b]
                rel = m.rel[:, bass.ds(t, 1), :].rearrange("p t j -> p (t j)")
                nc.vector.tensor_tensor(mask, m.iota[:, :].unsqueeze(1).to_broadcast([P, J, W]),
                                        rel.unsqueeze(2).to_broadcast([P, J, W]), ALU.is_equal).then_inc(mask_ready, 1)
                dve.wait_ge(mask_ready, masks + 1)
                if first:
                    w = m.w_edge[:, bass.ds(t * J, J)]
                    nc.vector.tensor_tensor(m.sel0[:, b], mask, w.unsqueeze(2).to_broadcast([P, J, W]),
                                            ALU.mult).then_inc(sel_ready, 1)
                else:
                    c = m.coef[:, bass.ds(t, 1), :, :].rearrange("p t j c -> p (t j) c")
                    nc.vector.tensor_tensor(m.sel[:, b], mask.unsqueeze(2).to_broadcast([P, J, 4, W]),
                                            c.unsqueeze(3).to_broadcast([P, J, 4, W]), ALU.mult).then_inc(sel_ready, 1)

            nc.vector.tensor_copy(m.iota[:, :], m.iota0[:, :])
            nc.vector.tensor_copy(m.base_f[:, :], m.base_bc[0:1, 0:SB])
            nc.vector.tensor_copy(m.base_i[:, :], m.base_bc[0:1, 0:SB]).then_inc(chain, 1)
            dve.wait_ge(chain, 1)
            select(0, 0, 0, 0)
            rounds = dve.value_load(m.rounds_i[0:1, 0:1], min_val=1, max_val=KROUND)
            with dve.Fori(0, rounds) as r:
                with dve.Fori(0, STEPS) as i:
                    for u in range(SLOTS):
                        g, t, b = r * SB + i * SLOTS + u, i * SLOTS + u, u % 2
                        base = dve.value_load(m.base_i[0:1, bass.ds(t, 1)], min_val=0, max_val=NPAD - W)
                        select(t + 1, 1 - b, g + 1, g + 1)
                        if first:
                            dve.wait_ge(rad_ready, g + 1)
                            dve.sem_inc(mark_d, 1)
                            nc.vector.tensor_tensor(m.coef[:, bass.ds(t, 1), :, :].rearrange("p t j c -> p (t j) c"),
                                                    m.attr[:, bass.ds(t, 1), :, :].rearrange("p t j c -> p (t j) c"),
                                                    radial[b].unsqueeze(2).to_broadcast([P, J, 4]), ALU.mult).then_inc(rad_sb, 1)
                        dve.wait_ge(added, g + 2)
                        dve.wait_ge(sumsT_ready, g + 1)
                        if first:
                            new = sumsT[b].rearrange("p (k n) -> p k n", n=W)
                        else:
                            new = bass.AP(tensor=m.ps[2 + b], offset=0, ap=[[512, P], [P + W, 4], [1, W]])
                            window = m.acc[:, 4, bass.ds(base, W)]
                            nc.vector.tensor_tensor(window, window, m.ps[2 + b][:, P:P + W], ALU.add)
                        window = accs[:, 0:3 if first else 4, bass.ds(base, W)]
                        nc.vector.tensor_tensor(window, window, new, ALU.add).then_inc(added, 1)
                dve.wait_ge(sel_ready, (r + 1) * SB + 1)
                nc.vector.tensor_scalar_add(m.iota[:, :], m.iota[:, :], float(W))
                nc.vector.tensor_scalar(m.base_f[:, :], m.base_f[:, :], float(W), float(NPAD - W),
                                        ALU.add, ALU.min).then_inc(chain, 1)
                dve.wait_ge(chain, 2 * r + 2)
                nc.vector.tensor_copy(m.base_i[:, :], m.base_f[:, :]).then_inc(chain, 1)
                dve.wait_ge(chain, 2 * r + 3)


def batch_factors(nc, m, dve, chain, at0, var_ready, std_ready, gamma, beta):
    for k in range(2):
        last = nc.vector.bn_aggr(m.mv[:, k, :], m.stats[:, k, :, :].rearrange("p c s -> p (c s)"))
    last.then_inc(var_ready, 1)
    dve.wait_ge(std_ready, 1)
    nc.vector.reciprocal(m.scale[:, :], m.tmp2[:, :]).then_inc(chain, 1)
    dve.wait_ge(chain, at0 + 1)
    nc.vector.tensor_tensor(m.scale[:, :], m.scale[:, :], m.bn_par[:, gamma, :], ALU.mult).then_inc(chain, 1)
    dve.wait_ge(chain, at0 + 2)
    nc.vector.tensor_tensor(m.tmp2[:, :], m.mv[:, :, 0], m.scale[:, :], ALU.mult).then_inc(chain, 1)
    dve.wait_ge(chain, at0 + 3)
    return nc.vector.tensor_tensor(m.shift[:, :], m.bn_par[:, beta, :], m.tmp2[:, :], ALU.subtract)


def second_product(nc, m, w):
    ctx = ExitStack()
    with ctx:
        (relu_ready, mm_ready, out_sb, stats_done, chain, deg_moved, norm_early, norm_late, w2_in, xh_in,
         deg_floor, deg_root, deg_ready, scale_ready, var1, std1,
         var2, std2, mark_d, mark_pe) = sems(nc, ctx, *("p_" + n for n in (
             "relu_ready", "mm_ready", "out_sb", "stats_done", "chain", "deg_moved", "norm_early", "norm_late",
             "w2_in", "xh_in", "deg_floor", "deg_root", "deg_ready",
             "scale_ready", "var1", "std1", "var2", "std2", "mark_d", "mark_pe")))
        block = ctx.enter_context(nc.Block())
        banks = [[m.ps[2 * b + k][:, 0:CH] for k in range(2)] for b in range(2)]
        assert NCH % 2 == 0

        def chunks(eng, step):
            step(0, 0, True, CH)
            step(1, 1, True, CH)
            with eng.Fori(1, NCH // 2 - 1) as s:
                for b in range(2):
                    step(2 * s + b, b, False, CH)
            step(NCH - 2, 0, False, CH)
            step(NCH - 1, 1, False, LAST)

        early = 2 * CH

        @block.sync
        def _(sp):
            sp.dma_start(m.deg_row, m.deg[0:1, :]).then_inc(deg_moved, 16)
            sp.dma_start(m.w2T, w["w2T"]).then_inc(w2_in, 16)
            sp.wait_ge(deg_moved, 16)
            sp.dma_start(m.deg_nodes[:, :], m.deg_row.rearrange("o (p n) -> (o p) n", p=P)).then_inc(deg_moved, 16)
            sp.wait_ge(deg_ready, 1)
            sp.dma_start(m.norm_row.rearrange("o (p n) -> (o p) n", p=P), m.deg_nodes[:, :]).then_inc(deg_moved, 16)
            sp.wait_ge(deg_moved, 48)
            sp.dma_start(m.deg[:, 0:early], m.norm_row[:, 0:early].to_broadcast([P, early])).then_inc(norm_early, 16)
            sp.dma_start(m.deg[:, early:NPAD], m.norm_row[:, early:NPAD].to_broadcast([P, NPAD - early])).then_inc(norm_late, 16)
            n = 2 * PAIRS // XH_LOADS
            for k in range(XH_LOADS):
                sp.dma_start(m.xh[:, n * k:n * (k + 1), :], m.xh_tab[n * k * P:n * (k + 1) * P, :].rearrange(
                    "(t p) f -> p t f", p=P)).then_inc(xh_in, 16)
            sp.wait_ge(xh_in, 16 * XH_LOADS)

        @block.gpsimd
        def _(pool):
            pool.wait_ge(deg_moved, 32)
            nc.gpsimd.tensor_scalar(m.deg_nodes[:, :], m.deg_nodes[:, :], 1.0, None, ALU.max).then_inc(deg_floor, 1)

        @block.tensor
        def _(pe):
            def step(c, b, first, real):
                pe.wait_ge(relu_ready, c + 1)
                if not first:
                    pe.wait_ge(out_sb, c - 1)
                pe.sem_inc(mark_pe, 1)
                for k in range(2):
                    for q in range(2):
                        last = nc.tensor.matmul(banks[b][k][:, 0:real], m.w2T[:, q, P * k:P * (k + 1)],
                                                m.agg3[:, q, bass.ds(c * CH, real)], start=(q == 0), stop=(q == 1))
                last.then_inc(mm_ready, 1)
            pe.wait_ge(w2_in, 16)
            chunks(pe, step)

        @block.scalar
        def _(act):
            act.wait_ge(deg_floor, 1)
            nc.scalar.activation(m.deg_nodes[:, :], m.deg_nodes[:, :], ACT.Sqrt).then_inc(deg_root, 1)
            act.wait_ge(var1, 1)
            nc.scalar.activation(m.tmp2[:, :], m.mv[:, :, 1], ACT.Sqrt, bias=m.eps_bn[:, 0:1]).then_inc(std1, 1)
            act.wait_ge(scale_ready, 1)

            def step(c, b, first, real):
                for k in range(2):
                    chunk = m.agg3[:, k, bass.ds(c * CH, real)]
                    last = nc.scalar.activation(chunk, chunk, ACT.Relu, bias=m.shift[:, k:k + 1], scale=m.scale[:, k:k + 1])
                last.then_inc(relu_ready, 1)
            chunks(act, step)
            act.wait_ge(var2, 1)
            nc.scalar.activation(m.tmp2[:, :], m.mv[:, :, 1], ACT.Sqrt, bias=m.eps_bn[:, 0:1]).then_inc(std2, 1)

        @block.vector
        def _(dve):
            def statistics(c, real):
                for k in range(2):
                    last = nc.vector.bn_stats(m.stats[:, k, bass.ds(c, 1), :].rearrange("p c s -> p (c s)"),
                                              m.agg3[:, k, bass.ds(c * CH, real)])
                return last

            with dve.Fori(0, NCH // 2) as c:
                statistics(c, CH)
            dve.wait_ge(deg_root, 1)
            nc.vector.reciprocal(m.deg_nodes[:, :], m.deg_nodes[:, :]).then_inc(deg_ready, 1)
            with dve.Fori(NCH // 2, NCH - 1) as c:
                statistics(c, CH)
            statistics(NCH - 1, LAST).then_inc(stats_done, 1)
            dve.wait_ge(stats_done, 1)
            batch_factors(nc, m, dve, chain, 0, var1, std1, 0, 1).then_inc(scale_ready, 1)

            def step(c, b, first, real):
                if at(c, 0):
                    dve.wait_ge(norm_early, 16)
                if at(c, 1):
                    dve.wait_ge(norm_late, 16)
                dve.wait_ge(mm_ready, c + 1)
                for k in range(2):
                    last = nc.vector.tensor_tensor(m.agg3[:, k, bass.ds(c * CH, real)], banks[b][k][:, 0:real],
                                                   m.deg[:, bass.ds(c * CH, real)], ALU.mult)
                last.then_inc(out_sb, 1)
                if not at(c, 0):
                    dve.wait_ge(out_sb, c)
                    dve.sem_inc(mark_d, 1)
                    statistics(c - 1, CH)
            chunks(dve, step)
            dve.wait_ge(out_sb, NCH)
            statistics(NCH - 1, LAST).then_inc(stats_done, 1)
            dve.wait_ge(stats_done, 2)
            batch_factors(nc, m, dve, chain, 3, var2, std2, 2, 3)


def between(nc, m):
    ctx = ExitStack()
    with ctx:
        x2_out, h2_out = (sems(nc, ctx, *(f"b_{n}{u}" for u in range(4))) for n in ("x2_out", "h2_out"))
        (relu_ready, turned, x2_ready, var_ready, std_ready, factors, h2_ready, moments, inverse, mark_pe, mark_a,
         mark_d, mark_s) = sems(nc, ctx, *("b_" + n for n in (
             "relu_ready", "turned", "x2_ready", "var_ready", "std_ready", "factors", "h2_ready", "moments",
             "inverse", "mark_pe", "mark_a", "mark_d", "mark_s")))
        block = ctx.enter_context(nc.Block())
        x2, h2, relu = m.tile_b, m.tile_a, m.y
        early = (0, 1, 2, 3)

        @block.sync
        def _(sp):
            def store_x2(i, u):
                sp.wait_ge(x2_ready, i + 1)
                sp.sem_inc(mark_s, 1)
                sp.dma_start(pair_rows(m.x2_tab, i), x2[:, u]).then_inc(x2_out[u], 16)

            def store_h2(i, u):
                sp.wait_ge(h2_ready, i + 1)
                sp.sem_inc(mark_s, 1)
                sp.dma_start(pair_rows(m.h2_tab, i), h2[:, u]).then_inc(h2_out[u], 16)

            def step(i, u, s, first):
                store_x2(i, u)
                if not first:
                    store_h2(i - 2, (u - 2) % 4)
            node_pairs(sp, step, peeled=4, unroll=4)
            store_h2(PAIRS - 2, (PAIRS - 2) % 4)
            store_h2(PAIRS - 1, (PAIRS - 1) % 4)
            for u in range(4):
                sp.wait_ge(x2_out[u], 16 * len(range(u, PAIRS, 4)))
                sp.wait_ge(h2_out[u], 16 * len(range(u, PAIRS, 4)))

        @block.scalar
        def _(act):
            def norm(i, u, stored):
                act.wait_ge(factors, i + 1)
                if stored is not None:
                    act.wait_ge(h2_out[u], 16 * stored)
                    act.sem_inc(mark_a, 1)
                for a in range(tiles_of(i)):
                    last = nc.scalar.activation(h2[:, u, a, :], x2[:, u, a, :], ACT.Relu,
                                                bias=m.nmr[:, u, a:a + 1], scale=m.rstd[:, u, a:a + 1])
                last.then_inc(h2_ready, 1)

            def step(i, u, s, first):
                if not first:
                    act.wait_ge(turned, i - 1)
                    act.sem_inc(mark_a, 1)
                for k in range(2):
                    last = nc.scalar.activation(relu[:, u % 2, k, :], m.agg3[:, k, bass.ds(i * (2 * P), 2 * P)], ACT.Relu,
                                                bias=m.shift[:, k:k + 1], scale=m.scale[:, k:k + 1])
                last.then_inc(relu_ready, 1)
                if not (first or at(i, 2)):
                    norm(i - 3, (u - 3) % 4, None if at(i, 3, 4, 5, 6) else s - (u < 3))
                if not first:
                    root(nc, m, act, var_ready, std_ready, i - 2, (u - 2) % 4)
            node_pairs(act, step, peeled=8, unroll=4)
            for i in range(PAIRS - 3, PAIRS):
                if i + 1 < PAIRS:
                    root(nc, m, act, var_ready, std_ready, i + 1, (i + 1) % 4)
                norm(i, i % 4, i // 4)

        @block.tensor
        def _(pe):
            def step(i, b, s, first):
                pe.wait_ge(relu_ready, i + 1)
                if not first:
                    pe.wait_ge(x2_ready, i - 1)
                pe.sem_inc(mark_pe, 1)
                for a in range(2):
                    for k in range(2):
                        last = nc.tensor.transpose(m.ps[b][:, D * a + P * k:D * a + P * (k + 1)],
                                                   relu[:, b, k, P * a:P * (a + 1)], m.ident[:, :])
                last.then_inc(turned, 1)
            node_pairs(pe, step)

        @block.vector
        def _(dve):
            nc.vector.tensor_copy(m.coef[:, SB, :, :], m.coef[:, 0, :, :])

            def factors_of(i, u, first):
                if not first:
                    dve.wait_ge(h2_ready, i - 3)
                norm_factors(nc, m, dve, inverse, std_ready, factors, i, u)

            def step(i, u, s, first):
                b = u % 2
                if not at(i, *early):
                    dve.wait_ge(h2_ready, i - 3)
                    dve.wait_ge(x2_out[u], 16 * s)
                dve.wait_ge(turned, i + 1)
                nc.vector.tensor_tensor(x2[:, u], m.ps[b][:, :].rearrange("p (a f) -> p a f", a=2),
                                        m.xh[:, bass.ds(2 * i, 2), :], ALU.add).then_inc(x2_ready, 1)
                if not first:
                    factors_of(i - 2, (u - 2) % 4, at(i, 2, 3, 4, 5))
                dve.wait_ge(x2_ready, i + 1)
                dve.sem_inc(mark_d, 1)
                variance(nc, m, dve, moments, var_ready, mark_d, i, u, x2[:, u])
            node_pairs(dve, step, peeled=8, unroll=4)
            for i in (PAIRS - 2, PAIRS - 1):
                factors_of(i, i % 4, False)

        @block.gpsimd
        def _(pool):
            nc.gpsimd.memset(m.acc[:, 2, :], 0.0)
            for k in range(5):
                pool.wait_ge(relu_ready, (k + 1) * PAIRS // 5)
                nc.gpsimd.memset(m.acc[:, 0:2, k * NPAD // 5:(k + 1) * NPAD // 5], 0.0)
                pool.wait_ge(x2_ready, (k + 1) * PAIRS // 5)
                nc.gpsimd.memset(m.xh[:, 2 * k * PAIRS // 5:2 * (k + 1) * PAIRS // 5, :], 0.0)


def output(nc, m, out):
    ctx = ExitStack()
    with ctx:
        x2_in = sems(nc, ctx, "o_x2_in0", "o_x2_in1")
        out_s = sems(nc, ctx, "o_out0", "o_out1")
        staged, mm_ready, y_ready, mark_a, mark_pe, mark_p = sems(
            nc, ctx, "o_staged", "o_mm", "o_y", "o_mark_a", "o_mark_pe", "o_mark_p")
        block = ctx.enter_context(nc.Block())
        stage = m.stage
        wk = m.wk[:, :, :].rearrange("p k (c o) -> p k c o", o=MUL)

        @block.sync
        def _(sp):
            def step(i, b, s, first):
                if not first:
                    sp.wait_ge(y_ready, i - 1)
                sp.dma_start(m.tile_a[:, b], pair_rows(m.x2_tab, i)).then_inc(x2_in[b], 16)
            node_pairs(sp, step)

        @block.scalar
        def _(act):
            def step(i, b, s, first):
                if not first:
                    act.wait_ge(mm_ready, i - 1)
                    act.sem_inc(mark_a, 1)
                nc.scalar.activation(stage[:, b], m.acc[:, :, bass.ds(i * (2 * P), 2 * P)], ACT.Copy).then_inc(staged, 1)
            node_pairs(act, step)

        @block.tensor
        def _(pe):
            def step(i, b, s, first):
                pe.wait_ge(staged, i + 1)
                if not first:
                    pe.wait_ge(y_ready, i - 1)
                pe.sem_inc(mark_pe, 1)
                for a in range(tiles_of(i)):
                    y = m.ps[b][:, D * a:D * (a + 1)].rearrange("p (c o) -> p c o", o=MUL)
                    for n, (k, c, every) in enumerate(((1, 0, 1), (0, 2, 1), (2, 1, 1), (3, 1, 2), (4, 0, 1))):
                        last = nc.tensor.matmul(y[:, c:c + every + 1:every, :], stage[:, b, k, P * a:P * (a + 1)],
                                                wk[:, k, c:c + every + 1:every, :], start=(n == 0), stop=(n == 4))
                last.then_inc(mm_ready, 1)
            node_pairs(pe, step)

        @block.vector
        def _(dve):
            def step(i, b, s, first):
                dve.wait_ge(x2_in[b], 16 * s + 16)
                dve.wait_ge(mm_ready, i + 1)
                if not first:
                    dve.wait_ge(out_s[b], 16 * s)
                n = tiles_of(i)
                nc.vector.tensor_tensor(m.tile_b[:, b, 0:n], m.tile_a[:, b, 0:n],
                                        m.ps[b][:, :].rearrange("p (a f) -> p a f", a=2)[:, 0:n],
                                        ALU.add).then_inc(y_ready, 1)
            node_pairs(dve, step)

        @block.gpsimd
        def _(pool):
            half = PAIRS // 2
            rest = N - (PAIRS - 1) * 2 * P

            def step(i, b, s, first):
                pool.wait_ge(y_ready, i + 1)
                pool.sem_inc(mark_p, 1)
                if isinstance(i, int) and i == PAIRS - 1:
                    assert rest <= P
                    pool.dma_start(out[i * 2 * P:N, :], m.tile_b[0:rest, b, 0, :]).then_inc(out_s[b], 16)
                else:
                    pool.dma_start(pair_rows(out, i), m.tile_b[:, b]).then_inc(out_s[b], 16)
            node_pairs(pool, step)
            pool.wait_ge(out_s[0], 16 * (half + 1))
            pool.wait_ge(out_s[1], 16 * half)


def build(nc, x, idx_rows, dst_rows, emb_rows, out, **w):
    ctx = ExitStack()
    with ctx:
        m = Memory(nc, ctx)
        prepare(nc, m, w, x, idx_rows, dst_rows, emb_rows)
        sweep(nc, m, 1, m.g_tab, idx_rows, emb_rows)
        second_product(nc, m, w)
        between(nc, m)
        sweep(nc, m, 2, m.h2_tab, idx_rows, emb_rows)
        output(nc, m, out)


def kernel(x, src, dst, edge_attr_10, edge_attr_4, edge_weight, L0_gnn_w1, L0_gnn_gamma1, L0_gnn_beta1, L0_gnn_w2,
           L0_gnn_eps_weight, L0_gnn_gamma_h, L0_gnn_beta_h, L1_gnn_w_00_0, L1_gnn_w_11_0, L1_gnn_w_01_1,
           L1_gnn_w_10_1, L1_gnn_fc_w1, L1_gnn_fc_w2):
    import numpy as np
    import concourse.bacc as bacc
    from concourse.bass_utils import run_bass_kernel_spmd

    def superblocked(a, fill=0):
        a = np.asarray(a).reshape(E, -1)
        a = np.pad(a, ((0, SB * SB_EDGES - E), (0, 0)), constant_values=fill)
        return a.reshape(SB, P, J, -1)

    def first_again(a):
        return np.concatenate([a, a[:SLOTS]], axis=0)

    def by_partition(a, again=True):
        if again:
            a = np.concatenate([a, a[:1]], axis=0)
        return np.swapaxes(a, 0, 1).reshape(P, -1)

    def halves(v):
        v = np.asarray(v)
        return np.swapaxes(v.reshape(2, P, -1), 0, 1)

    dst4 = superblocked(dst, FAR)
    fc1 = np.zeros((J * EMB, J * HID), np.float32)
    for j in range(J):
        fc1[EMB * j:EMB * (j + 1), HID * j:HID * (j + 1)] = L1_gnn_fc_w1
    fc2 = np.zeros((P, 2), np.float32)
    for j in range(2):
        fc2[HID * j:HID * (j + 1), j:j + 1] = L1_gnn_fc_w2
    weights = {"w_00_0": L1_gnn_w_00_0, "w_11_0": L1_gnn_w_11_0, "w_01_1": L1_gnn_w_01_1, "w_10_1": L1_gnn_w_10_1}
    wk = np.zeros((P, 5, D), np.float32)
    for k, part, column, name in WK_BLOCKS:
        wk[MUL * part:MUL * (part + 1), k, MUL * column:MUL * (column + 1)] = weights[name]
    arrays = {
        "x": np.pad(np.asarray(x)[:, FEATURES], ((0, NPAD - N), (0, 0))),
        "idx_rows": first_again(superblocked(src)[..., 0]),
        "dst_rows": dst4.reshape(SB, SB_EDGES),
        "dst_slots": by_partition(dst4),
        "emb_rows": first_again(superblocked(edge_attr_10).transpose(0, 2, 3, 1).reshape(SB, J * EMB, P)),
        "edge_attr_4": by_partition(superblocked(edge_attr_4), again=False),
        "edge_weight": by_partition(superblocked(edge_weight)),
        "w1T": halves(np.asarray(L0_gnn_w1).T[FEATURES, :]),
        "w2T": halves(np.asarray(L0_gnn_w2).T[:, FEATURES]),
        "bn_par": np.stack([halves(v)[..., 0] for v in (
            L0_gnn_gamma1, L0_gnn_beta1, np.asarray(L0_gnn_gamma_h)[FEATURES], np.asarray(L0_gnn_beta_h)[FEATURES])], axis=1),
        "eps": np.asarray(L0_gnn_eps_weight).reshape(1, 1),
        "fc1": fc1, "fc2": fc2, "wk": wk,
    }
    nc = bacc.Bacc("TRN2", target_bir_lowering=False, num_devices=1)
    given, args = {}, {}
    for name, a in arrays.items():
        a = np.ascontiguousarray(a)
        given[f"in_{name}"] = a
        args[name] = nc.dram_tensor(f"in_{name}", a.shape, mybir.dt.from_np(a.dtype), kind="ExternalInput").ap()
    out = nc.dram_tensor("out_y", (N, D), f32, kind="ExternalOutput").ap()
    build(nc, out=out, **args)
    r = run_bass_kernel_spmd(nc, [given], core_ids=[0])
    return np.ascontiguousarray(r.results[0]["out_y"][:, np.argsort(FEATURES)])
```
